# Optimizing a Trainium2 kernel written in Bass

```python
import numpy as np
import jax
import jax.numpy as jnp

def _softmax(x, axis=-1):
    return jax.nn.softmax(x, axis=axis)

def _gelu(x):
    return jax.nn.gelu(x, approximate=True)

def _silu(x):
    return jax.nn.silu(x)

def _sigmoid(x):
    return jax.nn.sigmoid(x)

def _layernorm(x, axis=-1, eps=1e-05):
    m = jnp.mean(x, axis=axis, keepdims=True)
    v = jnp.var(x, axis=axis, keepdims=True)
    return (x - m) / jnp.sqrt(v + eps)

def _scatter_add(tgt, idx, src, axis=0):
    return tgt.at[idx].add(src)

def _segment_sum(src, seg, n):
    return jax.ops.segment_sum(src, seg, n)
kernel_name = 'mk_gnn_preln_d1_gnn_r32_da4fb7'

def setup_inputs(seed: int=0):
    np.random.seed(seed)
    _w = jnp.asarray

    def _rec_inputs():
        import jax
        import jax.numpy as jnp
        _gk = jax.random.key(seed)
        x = -1.686e-05 + 1 * jax.random.normal(jax.random.fold_in(_gk, 1), (50000, 160), jnp.float32)
        src = jax.random.randint(jax.random.fold_in(_gk, 2), (50000,), 0, 50000, jnp.int32)
        dst = jnp.minimum((50000 * jax.random.uniform(jax.random.fold_in(_gk, 3), (50000,)) ** 2.0).astype(jnp.int32), 49999)
        _o = jnp.argsort(dst, stable=True)
        src = src[_o]
        dst = dst[_o]
        edge_attr_32 = 0.000196303 + 1.00016 * jax.random.normal(jax.random.fold_in(_gk, 11), (50000, 32), jnp.float32)
        node_vec1 = -0.00915711 + 0.999674 * jax.random.normal(jax.random.fold_in(_gk, 13), (50000, 1), jnp.float32)
        return (x, src, dst, edge_attr_32, node_vec1)
    x, src, dst, edge_attr_32, node_vec1 = _rec_inputs()

    def _L0_gnn_setup():
        import jax, jax.numpy as jnp
        import numpy as np
        MUL0_N, MUL1_N = (64, 32)
        MUL0_E, MUL1_E = (8, 8)
        MUL0_H, MUL1_H = (64, 32)
        N_NODES, N_EDGES = (50000, 25000)
        D_NODE = MUL0_N + 3 * MUL1_N
        D_EDGE = MUL0_E + 3 * MUL1_E
        D_HID = MUL0_H + 3 * MUL1_H

        def _split(x, mul0, mul1):
            s = x[..., :mul0]
            v = x[..., mul0:].reshape(x.shape[0], mul1, 3)
            return (s, v)

        def fctp_messages(x, e, W1, W2, W3, W4):
            xs, xv = _split(x, MUL0_N, MUL1_N)
            es, ev = _split(e, MUL0_E, MUL1_E)
            inv_sqrt2 = 1.0 / np.sqrt(2.0)
            s1 = jnp.einsum('ea,eb,abc->ec', xs, es, W1) * (1.0 / np.sqrt(MUL0_N * MUL0_E))
            s2 = jnp.einsum('eai,ebi,abc->ec', xv, ev, W2) * (1.0 / (np.sqrt(3.0) * np.sqrt(MUL1_N * MUL1_E)))
            out_s = (s1 + s2) * inv_sqrt2
            v1 = jnp.einsum('ea,ebi,abc->eci', xs, ev, W3) * (1.0 / np.sqrt(MUL0_N * MUL1_E))
            v2 = jnp.einsum('eai,eb,abc->eci', xv, es, W4) * (1.0 / np.sqrt(MUL1_N * MUL0_E))
            out_v = (v1 + v2) * inv_sqrt2
            return jnp.concatenate([out_s, out_v.reshape(out_v.shape[0], -1)], axis=-1)
        key = jax.random.key(seed)
        ks = jax.random.split(key, 12)
        node_features = jax.random.normal(ks[0], (N_NODES, D_NODE), dtype=jnp.float32)
        edge_index = jax.random.randint(ks[1], (2, N_EDGES), 0, N_NODES, dtype=jnp.int64)
        edge_attr_tensor = jax.random.normal(ks[2], (N_EDGES, D_EDGE), dtype=jnp.float32)
        node_attr_scalar_raw = jax.random.normal(ks[3], (N_NODES, 1), dtype=jnp.float32)
        W1 = jax.random.normal(ks[4], (MUL0_N, MUL0_E, MUL0_H), dtype=jnp.float32)
        W2 = jax.random.normal(ks[5], (MUL1_N, MUL1_E, MUL0_H), dtype=jnp.float32)
        W3 = jax.random.normal(ks[6], (MUL0_N, MUL1_E, MUL1_H), dtype=jnp.float32)
        W4 = jax.random.normal(ks[7], (MUL1_N, MUL0_E, MUL1_H), dtype=jnp.float32)
        Wm = jax.random.normal(ks[8], (D_HID, D_HID), dtype=jnp.float32) / np.sqrt(D_HID)
        bm = jnp.zeros((D_HID,), dtype=jnp.float32)
        Wu = jax.random.normal(ks[9], (D_NODE + D_HID, D_NODE), dtype=jnp.float32) / np.sqrt(D_NODE + D_HID)
        bu = jnp.zeros((D_NODE,), dtype=jnp.float32)
        return {'node_features': node_features, 'edge_index': edge_index, 'edge_attr_tensor': edge_attr_tensor, 'node_attr_scalar_raw': node_attr_scalar_raw, 'W1': W1, 'W2': W2, 'W3': W3, 'W4': W4, 'Wm': Wm, 'bm': bm, 'Wu': Wu, 'bu': bu}
    _L0_gnn_all = _L0_gnn_setup()
    _L0_gnn_in = {k: v for k, v in _L0_gnn_all.items() if k in ('W1', 'W2', 'W3', 'W4', 'Wm', 'bm', 'Wu', 'bu')}
    del _L0_gnn_all
    return {'x': x, 'src': src, 'dst': dst, 'edge_attr_32': edge_attr_32, 'node_vec1': node_vec1, 'L0_gnn_W1': _L0_gnn_in['W1'], 'L0_gnn_W2': _L0_gnn_in['W2'], 'L0_gnn_W3': _L0_gnn_in['W3'], 'L0_gnn_W4': _L0_gnn_in['W4'], 'L0_gnn_Wm': _L0_gnn_in['Wm'], 'L0_gnn_bm': _L0_gnn_in['bm'], 'L0_gnn_Wu': _L0_gnn_in['Wu'], 'L0_gnn_bu': _L0_gnn_in['bu']}

def reference(x, src, dst, edge_attr_32, node_vec1, L0_gnn_W1, L0_gnn_W2, L0_gnn_W3, L0_gnn_W4, L0_gnn_Wm, L0_gnn_bm, L0_gnn_Wu, L0_gnn_bu):
    import jax
    import jax.numpy as jnp

    def _L0_gnn_ref(node_features, edge_index, edge_attr_tensor, node_attr_scalar_raw, W1, W2, W3, W4, Wm, bm, Wu, bu):
        import jax, jax.numpy as jnp
        import numpy as np
        MUL0_N, MUL1_N = (64, 32)
        MUL0_E, MUL1_E = (8, 8)
        MUL0_H, MUL1_H = (64, 32)
        N_NODES, N_EDGES = (50000, 25000)
        D_NODE = MUL0_N + 3 * MUL1_N
        D_EDGE = MUL0_E + 3 * MUL1_E
        D_HID = MUL0_H + 3 * MUL1_H

        def _split(x, mul0, mul1):
            s = x[..., :mul0]
            v = x[..., mul0:].reshape(x.shape[0], mul1, 3)
            return (s, v)

        def fctp_messages(x, e, W1, W2, W3, W4):
            xs, xv = _split(x, MUL0_N, MUL1_N)
            es, ev = _split(e, MUL0_E, MUL1_E)
            inv_sqrt2 = 1.0 / np.sqrt(2.0)
            s1 = jnp.einsum('ea,eb,abc->ec', xs, es, W1) * (1.0 / np.sqrt(MUL0_N * MUL0_E))
            s2 = jnp.einsum('eai,ebi,abc->ec', xv, ev, W2) * (1.0 / (np.sqrt(3.0) * np.sqrt(MUL1_N * MUL1_E)))
            out_s = (s1 + s2) * inv_sqrt2
            v1 = jnp.einsum('ea,ebi,abc->eci', xs, ev, W3) * (1.0 / np.sqrt(MUL0_N * MUL1_E))
            v2 = jnp.einsum('eai,eb,abc->eci', xv, es, W4) * (1.0 / np.sqrt(MUL1_N * MUL0_E))
            out_v = (v1 + v2) * inv_sqrt2
            return jnp.concatenate([out_s, out_v.reshape(out_v.shape[0], -1)], axis=-1)
        row, col = (edge_index[0], edge_index[1])
        tp = fctp_messages(node_features[col], edge_attr_tensor, W1, W2, W3, W4)
        messages = tp @ Wm + bm
        agg = jax.ops.segment_sum(messages, row, num_segments=N_NODES)
        upd = jnp.concatenate([node_features, agg], axis=-1) @ Wu + bu
        return node_features + upd
    edge_index = jnp.stack([src, dst])
    h = jnp.maximum(_layernorm(x, axis=-1), 0.0)
    x = x + _L0_gnn_ref(h, edge_index, edge_attr_32, node_vec1, L0_gnn_W1, L0_gnn_W2, L0_gnn_W3, L0_gnn_W4, L0_gnn_Wm, L0_gnn_bm, L0_gnn_Wu, L0_gnn_bu)
    return x

_drawn_inputs = setup_inputs


def setup_inputs(seed=0):
    import zlib

    import numpy as np

    out = dict(_drawn_inputs(seed))
    spreads = {'L0_gnn_bm': (0.0, 0.1), 'L0_gnn_bu': (0.0, 0.1)}
    factors = {}
    for name, (base, spread) in spreads.items():
        noise = np.random.default_rng([zlib.crc32(name.encode()), seed]).standard_normal(out[name].shape)
        drawn = base * np.exp(spread * noise) if base else spread * noise
        out[name] = jnp.asarray(drawn.astype(out[name].dtype))
    for name, factor in factors.items():
        out[name] = (out[name] * factor).astype(out[name].dtype)
    return out
```

```python
import concourse.bass as bass
from concourse import mybir
from contextlib import ExitStack

F32 = mybir.dt.float32
BF16 = mybir.dt.bfloat16
I32 = mybir.dt.int32
ALU = mybir.AluOpType
ACT = mybir.ActivationFunctionType

N = 50000
S0, V0 = 64, 32
D = S0 + 3 * V0
EB = 8
DE = EB + 3 * EB
EPS = 1e-5

P = 128
G = 4
T = -(-N // (P * G)) * G
NB = T // G
NPAD = P * T
TAIL = N - (P - 1) * T
B_FULL = TAIL // G
SPLIT = 112
W = G * P
DUMP = N
assert TAIL % G == 0 and NPAD >= N + P

RING = 7
UNROLL = 2 * RING
assert NB % UNROLL == 0

ES64A, ES32, ES64B, EV0, EV1, EV2 = range(6)
STEPS = 6
CHUNKS = {ES64A: 2, ES32: 6, ES64B: 2, EV0: 4, EV1: 4, EV2: 4}
FIRST = {}
_at = 0
for _u in range(STEPS):
    FIRST[_u] = _at
    _at += CHUNKS[_u]
PRODUCTS = _at

XS, XV, Y3 = 0, 1, 4
OPERANDS = 6
AUX_STEP = {0: 0, 3: 1, 4: 2, 5: 3}
AUX = 4


class At:

    def __init__(self, i, u):
        self.g = i * UNROLL + u
        self.slot = u % RING
        self.par = u % 2
        self.turn = i * (UNROLL // RING) + u // RING


def after(k, n):
    return not isinstance(k, int) or k >= n


def pass_over_nodes(engine, *stages):
    for u in range(UNROLL):
        for j, stage in enumerate(stages[:u + 1]):
            stage(At(0, u - j))
    with engine.Fori(1, NB // UNROLL) as i:
        for u in range(UNROLL):
            for j, stage in enumerate(stages):
                stage(At(i, u - j))
    for u in range(len(stages) - 1):
        for j, stage in enumerate(stages):
            if j > u:
                stage(At(NB // UNROLL - 1, UNROLL + u - j))


def tp_message_passing(nc, x, src, dst, e, w1, w2, w3, w4, wm, bm, wu, bu, out):
    ctx = ExitStack()
    with ctx:
        def sb(name, shape, dt):
            return ctx.enter_context(nc.sbuf_tensor(name, shape, dt))

        def sem(name):
            return ctx.enter_context(nc.semaphore(name))

        h_dram = nc.dram_tensor("h_dram", (NPAD, D), F32, kind="Internal").ap()
        et_dram = nc.dram_tensor("et_dram", (NB * 3 * DE, W), BF16, kind="Internal").ap()

        ident = sb("ident", [P, P], F32)
        ident_b = sb("ident_b", [P, P], BF16)
        upto = sb("upto", [P, P], F32)
        pick = sb("pick", [3 * DE, DE], BF16)
        rep = sb("rep", [3 * DE, 12, P], BF16)
        sum_b = sb("sum_b", [P, V0], F32)
        dump_row = sb("dump_row", [P, 1], F32)
        w1c = sb("w1c", [P, 4, S0], F32)
        w2c = sb("w2c", [P, 2, S0], F32)
        w4c = sb("w4c", [P, 2, V0], F32)
        w3c = sb("w3c", [P, 2, P], F32)
        wma = sb("wma", [P, D], F32)
        wmb = sb("wmb", [P, D], F32)
        wmta = sb("wmta", [P, 2, P], F32)
        wmtb = sb("wmtb", [P, 2, P], F32)
        wub = sb("wub", [P, 2, D], F32)
        wfa = sb("wfa", [P, D], F32)
        wfb = sb("wfb", [P, D], F32)
        wta = sb("wta", [P, D], F32)
        wtb = sb("wtb", [P, D], F32)
        perm_a = sb("perm_a", [P, D], F32)
        perm_b = sb("perm_b", [V0, D], F32)

        src_i = sb("src_i", [P, NB, G], I32)
        dst_i = sb("dst_i", [P, NB, G], I32)
        part_i = sb("part_i", [P, 2, NB, G], I32)
        src_f = sb("src_f", [P, NB, 2, G], F32)
        src_b = sb("src_b", [P, NB, 2, G], BF16)

        x_s = sb("x_s", [P, RING, G, D], F32)
        z_s = sb("z_s", [P, 2, G, D], F32)
        h_s = sb("h_s", [P, RING, G, D], F32)
        base_s = sb("base_s", [P, RING, G, D], F32)
        e_s = sb("e_s", [P, RING, G, DE], F32)
        ep_s = sb("ep_s", [P, 2, G, 3, DE], BF16)
        er_s = sb("er_s", [P, 2, G, DE], F32)
        et_w = sb("et_w", [3 * DE, RING, W], BF16)
        stats = sb("stats", [P, 2, G, 6], F32)
        mv = sb("mv", [P, 2, G, 2], F32)
        std = sb("std", [P, 2, G], F32)
        rstd = sb("rstd", [P, 2, G], F32)
        eps = sb("eps", [P, 1], F32)
        hta = sb("hta", [P, 2, W], F32)
        htb = sb("htb", [P, 2, W], F32)

        et = sb("et", [3 * DE, 2, W], BF16)
        hg = sb("hg", [P, 2, G, D], F32)
        operand = sb("operand", [P, 2, OPERANDS, W], F32)
        prod = sb("prod", [P, PRODUCTS, W], F32)
        tpa = sb("tpa", [P, W], F32)
        tpb = sb("tpb", [P, W], F32)
        same = sb("same", [P, G, P], F32)
        count = sb("count", [P, G], F32)
        shift = sb("shift", [P, G], F32)
        m_s = sb("m_s", [P, G, D], F32)
        dd_s = sb("dd_s", [P, 2, G, D], F32)
        dst_slot = sb("dst_slot", [P, 2, G], I32)
        srcf_slot = sb("srcf_slot", [P, 2, 2, G], F32)
        srcb_slot = sb("srcb_slot", [P, 2, 2, G], BF16)
        row_slot = sb("row_slot", [P, 2, G], I32)

        ps = ctx.enter_context(nc.psum_tensor("ps", [P, 8, W], F32))
        n_et = ps[0:3 * DE, 7, 0:W // 2].bitcast(BF16)

        s_wload = sem("weights_loaded")
        s_iload = sem("indices_loaded")
        s_const = sem("pool_constants")
        s_prep = sem("vector_prep")
        s_wt_ps = sem("weights_transposed")
        s_wt_sb = sem("weights_copied")
        s_tables = sem("tables_ready")
        s_passed = sem("pool_waits_passed")
        s_passed_v = sem("vector_waits_passed")
        s_x = [sem(f"x_loaded{q}") for q in range(RING)]
        s_e = [sem(f"e_loaded{q}") for q in range(RING)]
        s_stat = sem("node_stats")
        s_var = sem("node_variance")
        s_std = sem("node_deviation")
        s_rstd = sem("node_inverse_deviation")
        s_z = sem("node_normalised")
        s_h = sem("node_relu")
        s_ht_ps = sem("node_transposed")
        s_ht = sem("node_transposed_copied")
        s_base_ps = sem("node_product")
        s_base = sem("node_base")
        s_split = sem("edge_split_chain")
        s_ep = sem("edge_split")
        s_et_ps = sem("edge_transposed")
        s_et = sem("edge_transposed_copied")
        s_hst = [sem(f"h_stored{q}") for q in range(RING)]
        s_bst = [sem(f"base_stored{q}") for q in range(RING)]
        s_est = [sem(f"et_stored{q}") for q in range(RING)]
        s_etl = [sem(f"et_loaded{q}") for q in range(2)]
        s_dslot = sem("dst_slot_ready")
        s_mslot = sem("src_slots_ready")
        s_gath = [sem(f"h_gathered{q}") for q in range(2)]
        s_rep = sem("edge_replicated")
        s_prod = sem("products_ready")
        s_contr = sem("products_contracted")
        s_aux = sem("aux_in_psum")
        s_auxc = sem("aux_copied")
        s_tp = sem("tensor_product_copied")
        s_row = sem("source_row_in_psum")
        s_md = sem("messages_in_psum")
        s_mdc = sem("messages_copied")
        s_dve = sem("vector_owner_chain")
        s_same = sem("same_source_ready")
        s_scat = sem("scattered")

        def rows(ap, p0, p1, width, g):
            return ap.rearrange("(p t) c -> p (t c)", t=T)[p0:p1, bass.ds(g * (G * width), G * width)]

        x_head = x[0:(P - 1) * T, :]
        e_head = e[0:(P - 1) * T, :]

        def tail_rows(ap, width, g):
            return ap[(P - 1) * T:N, :].rearrange("(p t) c -> p (t c)", p=1)[:, bass.ds(g * (G * width), G * width)]

        N_WLOAD = [0]

        block = ctx.enter_context(nc.Block())

        @block.sync
        def _(sp):
            for table, flat in ((src_i, src), (dst_i, dst)):
                if table is src_i:
                    sp.wait_ge(s_prep, 2)
                v = table[:, :, :].rearrange("p b g -> p (b g)")
                head = flat[0:(P - 1) * T].rearrange("(p t) -> p t", t=T)
                sp.dma_start(v[0:SPLIT, :], head[0:SPLIT, :]).then_inc(s_iload, 16)
                sp.dma_start(v[SPLIT:P - 1, :], head[SPLIT:P - 1, :]).then_inc(s_iload, 16)
                sp.dma_start(v[P - 1:P, 0:TAIL], flat[(P - 1) * T:N].rearrange("(p t) -> p t", p=1)).then_inc(s_iload, 16)

            def load(g, q, full):
                for dst_t, head, whole, width, s in ((x_s, x_head, x, D, s_x), (e_s, e_head, e, DE, s_e)):
                    d = dst_t[:, q].rearrange("p g c -> p (g c)")
                    sp.dma_start(d[0:SPLIT, :], rows(head, 0, SPLIT, width, g)).then_inc(s[q], 16)
                    sp.dma_start(d[SPLIT:P - 1, :], rows(head, SPLIT, P - 1, width, g)).then_inc(s[q], 16)
                    if full:
                        sp.dma_start(d[P - 1:P, :], tail_rows(whole, width, g)).then_inc(s[q], 16)
                    else:
                        sp.sem_inc(s[q], 16)

            def store(g, q):
                sp.wait_ge(s_h, g + 1)
                sp.dma_start(rows(h_dram, 0, P, D, g), h_s[:, q].rearrange("p g c -> p (g c)")).then_inc(s_hst[q], 16)
                sp.wait_ge(s_et, g + 1)
                sp.dma_start(et_dram[bass.ds(g * (3 * DE), 3 * DE), :], et_w[:, q, :]).then_inc(s_est[q], 16)
                sp.wait_ge(s_base, g + 1)
                sp.dma_start(rows(out, 0, P, D, g), base_s[:, q].rearrange("p g c -> p (g c)")).then_inc(s_bst[q], 16)

            AHEAD = 3

            def node_block(g, q, full):
                load(g + AHEAD, (q + AHEAD) % RING, full)
                store(g, q)

            sp.wait_ge(s_prep, 4)
            for g in range(AHEAD):
                load(g, g, True)
            for g in range(RING):
                node_block(g, g, True)
            with sp.Fori(1, 7) as i:
                for q in range(RING):
                    node_block(i * RING + q, q, True)
            for g in range(7 * RING, 8 * RING):
                node_block(g, g % RING, g + AHEAD < B_FULL)
            with sp.Fori(8, NB // RING - 1) as i:
                for q in range(RING):
                    node_block(i * RING + q, q, False)
            for g in range(NB - RING, NB):
                if g + AHEAD < NB:
                    node_block(g, g % RING, False)
                else:
                    store(g, g % RING)

            for q in range(RING):
                sp.wait_ge(s_est[q], 16 * (NB // RING))

            def load_et(k, q):
                sp.dma_start(et[:, q, :], et_dram[bass.ds(k * (3 * DE), 3 * DE), :]).then_inc(s_etl[q], 16)

            load_et(0, 0)
            load_et(1, 1)
            with sp.Fori(1, NB // 2) as i:
                for q in range(2):
                    k = i * 2 + q
                    sp.wait_ge(s_rep, (k - 2) * STEPS + STEPS)
                    load_et(k, q)

        @block.gpsimd
        def _(pool):
            pool.memset(ident[:, :], 0.0).then_inc(s_const, 1)
            pool.memset(ident_b[:, :], 0.0).then_inc(s_const, 1)
            pool.memset(pick[:, :], 0.0).then_inc(s_const, 1)
            pool.memset(sum_b[:, :], 0.0).then_inc(s_const, 1)
            pool.memset(upto[:, :], 1.0).then_inc(s_const, 1)
            pool.iota(dump_row[:, :], [[0, 1]], base=DUMP, channel_multiplier=1,
                      allow_small_or_imprecise_dtypes=True).then_inc(s_const, 1)
            pool.wait_ge(s_const, 6)
            for m in (ident, ident_b):
                pool.affine_select(out=m[:, :], in_=m[:, :], compare_op=ALU.not_equal, fill=1.0, base=0,
                                   pattern=[[-1, P]], channel_multiplier=1).then_inc(s_const, 1)
            pool.affine_select(out=upto[:, :], in_=upto[:, :], compare_op=ALU.is_ge, fill=0.0, base=0,
                               pattern=[[-1, P]], channel_multiplier=1).then_inc(s_const, 1)
            for n in range(3):
                pool.affine_select(out=pick[:, :], in_=pick[:, :], compare_op=ALU.not_equal, fill=1.0, base=-DE * n,
                                   pattern=[[-1, DE]], channel_multiplier=1).then_inc(s_const, 1)
                pool.wait_ge(s_const, 10 + n)
            for n in range(4):
                pool.affine_select(out=sum_b[:, :], in_=sum_b[:, :], compare_op=ALU.not_equal, fill=1.0, base=-V0 * n,
                                   pattern=[[-1, V0]], channel_multiplier=1).then_inc(s_const, 1)
                pool.wait_ge(s_const, 13 + n)

            def wait(s, value):
                pool.wait_ge(s, value)
                pool.sem_inc(s_passed, 1)

            def split(b):
                def link(ins, n):
                    ins.then_inc(s_split, 1)
                    wait(s_split, b.g * 4 + n)
                wait(s_e[b.slot], (b.turn + 1) * 48)
                if after(b.g, 2):
                    wait(s_et_ps, b.g - 1)
                part, rest, e_in = ep_s[:, b.par], er_s[:, b.par], e_s[:, b.slot]
                link(pool.tensor_copy(part[:, :, 0, :], e_in), 1)
                link(pool.tensor_tensor(rest, e_in, part[:, :, 0, :], ALU.subtract), 2)
                link(pool.tensor_copy(part[:, :, 1, :], rest), 3)
                link(pool.tensor_tensor(rest, rest, part[:, :, 1, :], ALU.subtract), 4)
                pool.tensor_copy(part[:, :, 2, :], rest).then_inc(s_ep, 1)

            pass_over_nodes(pool, split)

            def gather(k, q, t):
                pool.indirect_dma_start(
                    out=hg[:, q, t, :], out_offset=None, in_=h_dram,
                    in_offset=bass.IndirectOffsetOnAxis(ap=dst_slot[:, q, t:t + 1], axis=0),
                ).then_inc(s_gath[q], 16)

            def scatter(k, q, t):
                if t in (0, 2):
                    wait(s_mdc, k * 4 + 3 + t // 2)
                if after(k, 1) or t > 0:
                    wait(s_scat, k * (G * 16) + t * 16)
                pool.indirect_dma_start(
                    out=out, out_offset=bass.IndirectOffsetOnAxis(ap=row_slot[:, q, t:t + 1], axis=0),
                    in_=dd_s[:, q, t, :], in_offset=None, compute_op=ALU.add,
                ).then_inc(s_scat, 16)

            for q in range(RING):
                pool.wait_ge(s_hst[q], 16 * (NB // RING))
            for k in range(2):
                wait(s_dslot, k + 1)
                for t in range(G):
                    gather(k, k, t)
            for q in range(RING):
                pool.wait_ge(s_bst[q], 16 * (NB // RING))

            def edge_block(k, q, with_gather=True):
                if with_gather:
                    wait(s_aux, k * AUX + 2)
                    wait(s_dslot, k + 3)
                if after(k, 2):
                    wait(s_same, k - 1)
                for t in range(G):
                    if with_gather:
                        gather(k + 2, q, t)
                    if after(k, 2):
                        scatter(k - 2, q, t)

            for k in range(4):
                edge_block(k, k % 2)
            with pool.Fori(2, NB // 2 - 1) as i:
                for q in range(2):
                    edge_block(i * 2 + q, q)
            for k in range(NB - 2, NB + 2):
                edge_block(k, k % 2, with_gather=False)
            pool.wait_ge(s_scat, NB * G * 16)

        @block.scalar
        def _(act):
            def ld(dst_ap, src_ap):
                act.dma_start(dst_ap, src_ap).then_inc(s_wload, 16)
                N_WLOAD[0] += 16

            act.wait_ge(s_prep, 1)
            for b in range(EB):
                ld(w1c[S0 * (b % 2):S0 * (b % 2 + 1), b // 2, :], w1[:, b, :])
                ld(w2c[V0 * (b % 4):V0 * (b % 4 + 1), b // 4, :], w2[:, b, :])
                ld(w4c[V0 * (b % 4):V0 * (b % 4 + 1), b // 4, :], w4[:, b, :])
            ld(w3c[0:S0, :, :], w3.rearrange("a (j b) c -> a j (b c)", j=2))

            def in_order(dst_a, dst_b, mat):
                vec = mat[S0:D, :].rearrange("(c i) n -> c i n", i=3)
                ld(dst_a[0:S0, :], mat[0:S0, :])
                ld(dst_a[S0:S0 + V0, :], vec[:, 0, :])
                ld(dst_a[S0 + V0:P, :], vec[:, 1, :])
                ld(dst_b[0:V0, :], vec[:, 2, :])

            in_order(wma, wmb, wm)
            ld(wmb[V0:V0 + 1, :], bm.rearrange("(o n) -> o n", o=1))
            ld(wmb[S0:P, :], wm[0:S0, :])
            in_order(wta, wtb, wu[0:D, :])
            ld(wtb[V0:V0 + 1, :], bu.rearrange("(o n) -> o n", o=1))
            ld(wub[:, 0, :], wu[D:D + P, :])
            ld(wub[0:D - P, 1, :], wu[D + P:2 * D, :])

            act.wait_ge(s_wt_ps, 1)
            nc.scalar.activation(wmta[:, :, :], ps[:, 0, 0:2 * P].rearrange("p (a b) -> p a b", a=2), ACT.Copy)
            nc.scalar.activation(wmtb[0:V0, :, :], ps[0:V0, 1, 0:2 * P].rearrange("p (a b) -> p a b", a=2),
                                 ACT.Copy).then_inc(s_wt_sb, 1)
            act.wait_ge(s_wt_ps, 2)
            nc.scalar.activation(wfa[:, :], ps[:, 2, 0:D], ACT.Copy)
            nc.scalar.activation(wfb[:, :], ps[:, 3, 0:D], ACT.Copy).then_inc(s_wt_sb, 1)

            def deviation(b):
                act.wait_ge(s_var, b.g + 1)
                if after(b.g, 2):
                    act.wait_ge(s_rstd, b.g - 1)
                nc.scalar.activation(std[:, b.par, :], mv[:, b.par, :, 1], ACT.Sqrt, bias=eps[:, 0:1],
                                     scale=1.0).then_inc(s_std, 1)

            def relu(b):
                act.wait_ge(s_z, b.g + 1)
                if after(b.g, RING):
                    act.wait_ge(s_hst[b.slot], b.turn * 16)
                nc.scalar.activation(h_s[:, b.slot, :, 0:S0], z_s[:, b.par, :, 0:S0], ACT.Relu)
                for i3 in range(3):
                    last = nc.scalar.activation(
                        h_s[:, b.slot, :, S0 + V0 * i3:S0 + V0 * (i3 + 1)],
                        z_s[:, b.par, :, S0:D].rearrange("p g (c i) -> p g c i", i=3)[:, :, :, i3], ACT.Relu)
                last.then_inc(s_h, 1)

            def copy_transposed(b):
                act.wait_ge(s_ht_ps, b.g + 1)
                if after(b.g, 2):
                    act.wait_ge(s_base_ps, b.g - 1)
                nc.scalar.activation(hta[:, b.par, :], ps[:, b.par, :], ACT.Copy)
                nc.scalar.activation(htb[0:V0, b.par, :], ps[0:V0, 2, :], ACT.Copy).then_inc(s_ht, 1)
                act.wait_ge(s_et_ps, b.g + 1)
                if after(b.g, RING):
                    act.wait_ge(s_est[b.slot], b.turn * 16)
                nc.scalar.activation(et_w[:, b.slot, :], n_et, ACT.Copy).then_inc(s_et, 1)

            pass_over_nodes(act, deviation, relu, copy_transposed)

            act.wait_ge(s_tables, 1)

            def slot_dst(k, q):
                nc.scalar.activation(dst_slot[:, q, :], dst_i[:, bass.ds(k, 1), :].rearrange("p b g -> p (b g)"),
                                     ACT.Copy).then_inc(s_dslot, 1)

            def slot_src(k, q):
                nc.scalar.activation(srcf_slot[:, q].rearrange("p a g -> p (a g)"),
                                     src_f[:, bass.ds(k, 1)].rearrange("p b a g -> p (b a g)"), ACT.Copy)
                nc.scalar.activation(srcb_slot[:, q].rearrange("p a g -> p (a g)"),
                                     src_b[:, bass.ds(k, 1)].rearrange("p b a g -> p (b a g)"), ACT.Copy).then_inc(s_mslot, 1)

            def copy_aux(k, q, n):
                act.wait_ge(s_aux, k * AUX + n + 1)
                if n == 0:
                    for r in range(2):
                        last = nc.scalar.activation(operand[S0 * r:S0 * (r + 1), q, XS, :], ps[0:S0, 6, :], ACT.Copy)
                    for i3 in range(2):
                        for r in range(4):
                            last = nc.scalar.activation(operand[V0 * r:V0 * (r + 1), q, XV + i3, :],
                                                        ps[S0 + V0 * i3:S0 + V0 * (i3 + 1), 6, :], ACT.Copy)
                elif n == 1:
                    for r in range(4):
                        last = nc.scalar.activation(operand[V0 * r:V0 * (r + 1), q, XV + 2, :], ps[0:V0, 6, :], ACT.Copy)
                else:
                    last = nc.scalar.activation(operand[:, q, Y3 + n - 2, :], ps[:, 6, :], ACT.Copy)
                last.then_inc(s_auxc, 1)

            def copy_md(k, q, n):
                act.wait_ge(s_md, k * 4 + n + 1)
                if n == 2 and after(k, 2):
                    act.wait_ge(s_scat, (k - 1) * (G * 16))
                j = n % 2
                dest = m_s[:, 2 * j:2 * j + 2, :] if n < 2 else dd_s[:, q, 2 * j:2 * j + 2, :]
                nc.scalar.activation(dest, ps[:, 7, 0:2 * D].rearrange("p (a b) -> p a b", a=2), ACT.Copy).then_inc(s_mdc, 1)

            def copy_tp(k):
                act.wait_ge(s_contr, k * STEPS + STEPS)
                if after(k, 1):
                    act.wait_ge(s_md, (k - 1) * 4 + 2)
                nc.scalar.activation(tpa[:, :], ps[:, 4, :], ACT.Copy)
                nc.scalar.activation(tpb[0:V0, :], ps[0:V0, 5, :], ACT.Copy)
                nc.scalar.activation(tpb[S0:P, :], ps[S0:P, 5, :], ACT.Copy).then_inc(s_tp, 1)

            def edge_block(k, q, nxt=True, nxt2=True):
                o = 1 - q
                prev = after(k, 1)
                if prev:
                    copy_tp(k - 1)
                if after(k, 2):
                    act.wait_ge(s_same, k - 1)
                slot_src(k, q)
                if nxt2:
                    act.wait_ge(s_aux, k * AUX + 2)
                    slot_dst(k + 2, q)
                if nxt and prev:
                    act.wait_ge(s_prod, k * STEPS)
                for n in range(4):
                    if nxt:
                        copy_aux(k + 1, o, n)
                    if prev:
                        copy_md(k - 1, o, n)

            slot_dst(0, 0)
            slot_dst(1, 1)
            for n in range(AUX):
                copy_aux(0, 0, n)
            for k in range(4):
                edge_block(k, k % 2)
            with act.Fori(2, NB // 2 - 1) as i:
                for q in range(2):
                    edge_block(i * 2 + q, q)
            edge_block(NB - 2, 0, nxt2=False)
            edge_block(NB - 1, 1, nxt=False, nxt2=False)
            copy_tp(NB - 1)
            for n in range(4):
                copy_md(NB - 1, 1, n)

        @block.vector
        def _(dve):
            v = nc.vector
            for m in (w3c[:, :, :], wmb[:, :], wub[:, :, :], wtb[:, :], wmtb[:, :, :]):
                last = v.memset(m, 0.0)
            last.then_inc(s_prep, 1)
            v.memset(dst_i[:, :, :], 0)
            v.memset(eps[:, :], EPS)
            v.memset(tpb[:, :], 0.0)
            dve.wait_ge(s_const, 6)
            v.tensor_scalar(src_i[:, :, :].rearrange("p b g -> p (b g)"),
                            dump_row[:, 0:1].to_broadcast([P, T]), 0.0, None, ALU.add).then_inc(s_prep, 1)
            v.memset(htb[:, :, :], 0.0).then_inc(s_prep, 1)
            v.memset(x_s[:, :, :, :], 0.0)
            v.memset(e_s[:, :, :, :], 0.0).then_inc(s_prep, 1)
            dve.wait_ge(s_prep, 4)
            v.memset(tpb[V0:V0 + 1, :], 1.0)
            v.memset(htb[V0:V0 + 1, :, :], 1.0).then_inc(s_prep, 1)

            dve.wait_ge(s_const, 12)
            for r in range(12):
                if r < 4:
                    cols, n = pick[:, 2 * r:2 * r + 2], S0
                elif r < 6:
                    cols, n = pick[:, 4 * (r - 4):4 * (r - 4) + 4], V0
                else:
                    i3, j = (r - 6) // 2, (r - 6) % 2
                    cols, n = pick[:, EB:DE].rearrange("k (b i) -> k i b", i=3)[:, i3, 4 * j:4 * j + 4], V0
                v.tensor_copy(rep[:, r, :].rearrange("k (b a) -> k b a", a=n),
                              cols[:, :, None].to_broadcast([3 * DE, P // n, n]))

            dve.wait_ge(s_wload, N_WLOAD[0])
            half = 0.5 ** 0.5
            for m, scale in ((w1c, (S0 * EB) ** -0.5 * half), (w2c, (3.0 * V0 * EB) ** -0.5 * half),
                             (w4c, (V0 * EB) ** -0.5 * half), (w3c, (S0 * EB) ** -0.5 * half)):
                v.tensor_scalar(m[:, :, :], m[:, :, :], scale, None, ALU.mult)
            v.memset(perm_a[:, :], 0.0)
            v.memset(perm_b[:, :], 0.0).then_inc(s_prep, 1)
            dve.wait_ge(s_prep, 6)
            dve.wait_ge(s_const, 9)
            v.tensor_copy(perm_a[0:S0, 0:S0], ident[0:S0, 0:S0])
            for i3, (m, r0) in enumerate(((perm_a, S0), (perm_a, S0 + V0), (perm_b, 0))):
                last = v.tensor_copy(m[r0:r0 + V0, S0:D].rearrange("r (c i) -> r i c", i=3)[:, i3, :],
                                     ident[r0:r0 + V0, r0:r0 + V0])
            last.then_inc(s_prep, 1)
            dve.wait_ge(s_prep, 7)
            v.tensor_tensor(wta[:, :], wta[:, :], perm_a[:, :], ALU.add)
            v.tensor_tensor(wtb[0:V0, :], wtb[0:V0, :], perm_b[:, :], ALU.add).then_inc(s_prep, 1)

            dve.wait_ge(s_iload, 96)
            v.tensor_copy(src_f[:, :, 0, :], src_i[:, :, :])
            v.tensor_scalar(part_i[:, 0], src_i[:, :, :], 8, 8, ALU.logical_shift_right, ALU.logical_shift_left)
            v.tensor_scalar(part_i[:, 1], src_i[:, :, :], 255, None, ALU.bitwise_and).then_inc(s_prep, 1)
            dve.wait_ge(s_prep, 9)
            v.tensor_scalar(src_f[:, :, 1, :], src_f[:, :, 0, :], -1.0, dump_row[:, 0:1], ALU.mult, ALU.add)
            v.tensor_copy(src_b[:, :, 0, :], part_i[:, 0])
            v.tensor_copy(src_b[:, :, 1, :], part_i[:, 1]).then_inc(s_tables, 1)

            def statistics(b):
                dve.wait_ge(s_x[b.slot], (b.turn + 1) * 48)
                for t in range(G):
                    last = v.bn_stats(out=stats[:, b.par, t, :], in_=x_s[:, b.slot, t, :])
                last.then_inc(s_stat, 1)
                dve.wait_ge(s_stat, b.g + 1)
                dve.sem_inc(s_passed_v, 1)
                for t in range(G):
                    last = v.bn_aggr(out=mv[:, b.par, t, :], in_=stats[:, b.par, t, :])
                last.then_inc(s_var, 1)

            def normalise(b):
                dve.wait_ge(s_std, b.g + 1)
                v.reciprocal(rstd[:, b.par, :], std[:, b.par, :]).then_inc(s_rstd, 1)
                dve.wait_ge(s_rstd, b.g + 1)
                if after(b.g, 2):
                    dve.wait_ge(s_h, b.g - 1)
                for t in range(G):
                    last = v.tensor_scalar(z_s[:, b.par, t, :], x_s[:, b.slot, t, :], mv[:, b.par, t, 0:1],
                                           rstd[:, b.par, t:t + 1], ALU.subtract, ALU.mult)
                last.then_inc(s_z, 1)

            def add_base(b):
                dve.wait_ge(s_base_ps, b.g + 1)
                if after(b.g, RING):
                    dve.wait_ge(s_bst[b.slot], b.turn * 16)
                for j in range(2):
                    last = v.tensor_tensor(base_s[:, b.slot, 2 * j:2 * j + 2, :],
                                           ps[:, 3 + 2 * b.par + j, 0:2 * D].rearrange("p (a b) -> p a b", a=2),
                                           x_s[:, b.slot, 2 * j:2 * j + 2, :], ALU.add)
                last.then_inc(s_base, 1)

            pass_over_nodes(dve, statistics, normalise, add_base)

            def products(k, q, u):
                dve.wait_ge(s_rep, k * STEPS + u + 1)
                if u == 0:
                    dve.wait_ge(s_auxc, (k + 1) * AUX)
                if after(k, 1):
                    dve.wait_ge(s_contr, (k - 1) * STEPS + u + 1)
                pair = ps[:, 2 * (u % 2):2 * (u % 2) + 2, :]
                op = operand[:, q]
                f = FIRST[u]
                if u in (ES64A, ES64B):
                    last = v.tensor_tensor(prod[:, f:f + 2, :], op[:, XS:XS + 1, :].to_broadcast([P, 2, W]), pair, ALU.mult)
                elif u == ES32:
                    for j in range(2):
                        last = v.tensor_tensor(prod[:, f + 3 * j:f + 3 * j + 3, :], op[:, XV:XV + 3, :],
                                               pair[:, j:j + 1, :].to_broadcast([P, 3, W]), ALU.mult)
                else:
                    i3 = u - EV0
                    v.tensor_tensor(prod[:, f:f + 2, :], op[:, XV + i3:XV + i3 + 1, :].to_broadcast([P, 2, W]),
                                    pair, ALU.mult)
                    last = v.tensor_tensor(prod[:, f + 2:f + 4, :], op[:, Y3:Y3 + 2, :], pair, ALU.mult)
                last.then_inc(s_prod, 1)

            def owners(k, q):
                dve.wait_ge(s_row, k + 1)
                dve.wait_ge(s_mslot, k + 1)
                if after(k, 1):
                    dve.wait_ge(s_md, (k - 1) * 4 + 4)
                for t in range(G):
                    last = v.scalar_tensor_tensor(out=same[:, t, :], in0=ps[:, 7, P * t:P * (t + 1)],
                                                  scalar=srcf_slot[:, q, 0, t:t + 1], in1=upto[:, :],
                                                  op0=ALU.is_equal, op1=ALU.mult, accum_out=count[:, t:t + 1])
                last.then_inc(s_dve, 1)
                dve.wait_ge(s_dve, k * 2 + 1)
                v.scalar_tensor_tensor(out=shift[:, :], in0=count[:, :], scalar=1.5, in1=srcf_slot[:, q, 1, :],
                                       op0=ALU.is_gt, op1=ALU.mult).then_inc(s_dve, 1)
                dve.wait_ge(s_dve, k * 2 + 2)
                if after(k, 2):
                    dve.wait_ge(s_scat, (k - 1) * (G * 16))
                v.tensor_tensor(row_slot[:, q, :], shift[:, :], srcf_slot[:, q, 0, :], ALU.add).then_inc(s_same, 1)

            def edge_block(k, q):
                products(k, q, 0)
                if after(k, 1):
                    owners(k - 1, 1 - q)
                for u in range(1, STEPS):
                    products(k, q, u)

            for k in range(4):
                edge_block(k, k % 2)
            with dve.Fori(2, NB // 2) as i:
                for q in range(2):
                    edge_block(i * 2 + q, q)
            owners(NB - 1, 1)

        @block.tensor
        def _(pe):
            mm = nc.tensor.matmul
            pe.wait_ge(s_wload, N_WLOAD[0])
            pe.wait_ge(s_const, 16)
            for n, m in enumerate((wma, wmb)):
                nc.tensor.transpose(ps[:, 0, P * n:P * (n + 1)], m[:, 0:P], ident[:, :])
                last = nc.tensor.transpose(ps[0:D - P, 1, P * n:P * (n + 1)], m[:, P:D], ident[:, :])
            last.then_inc(s_wt_ps, 1)
            pe.wait_ge(s_wt_sb, 1)
            for n in range(2):
                mm(ps[:, 2 + n, 0:D], wmta[:, n, :], wub[:, 0, :], start=True, stop=False)
                last = mm(ps[:, 2 + n, 0:D], wmtb[:, n, :], wub[:, 1, :], start=False, stop=True)
            last.then_inc(s_wt_ps, 1)
            pe.wait_ge(s_wt_sb, 2)
            pe.wait_ge(s_prep, 8)

            def transposes(b):
                pe.wait_ge(s_h, b.g + 1)
                if after(b.g, 1):
                    pe.wait_ge(s_ht, b.g)
                for t in range(G):
                    nc.tensor.transpose(ps[:, b.par, P * t:P * (t + 1)], h_s[:, b.slot, t, 0:P], ident[:, :])
                for t in range(G):
                    last = nc.tensor.transpose(ps[0:V0, 2, P * t:P * (t + 1)], h_s[:, b.slot, t, P:D], ident[:, :])
                last.then_inc(s_ht_ps, 1)
                pe.wait_ge(s_ep, b.g + 1)
                if after(b.g, 1):
                    pe.wait_ge(s_et, b.g)
                for t in range(G):
                    last = nc.tensor.transpose(n_et[:, P * t:P * (t + 1)],
                                               ep_s[:, b.par, t].rearrange("p a b -> p (a b)"), ident_b[:, :])
                last.then_inc(s_et_ps, 1)

            def product(b):
                pe.wait_ge(s_ht, b.g + 1)
                if after(b.g, 2):
                    pe.wait_ge(s_base, b.g - 1)
                for t in range(G):
                    o = ps[:, 3 + 2 * b.par + t // 2, D * (t % 2):D * (t % 2 + 1)]
                    mm(o, hta[:, b.par, P * t:P * (t + 1)], wta[:, :], start=True, stop=False)
                    last = mm(o, htb[:, b.par, P * t:P * (t + 1)], wtb[:, :], start=False, stop=True)
                last.then_inc(s_base_ps, 1)

            pass_over_nodes(pe, transposes, product)

            pe.wait_ge(s_base, NB)
            pe.wait_ge(s_et, NB)

            def aux(k, q, c, n):
                if after(k, 1) or n > 0:
                    pe.wait_ge(s_auxc, k * AUX + n)
                if n == 0:
                    pe.wait_ge(s_gath[q], (c + 1) * (G * 16))
                    for t in range(G):
                        r = nc.tensor.transpose(ps[:, 6, P * t:P * (t + 1)], hg[:, q, t, 0:P], ident[:, :])
                elif n == 1:
                    for t in range(G):
                        r = nc.tensor.transpose(ps[0:V0, 6, P * t:P * (t + 1)], hg[:, q, t, P:D], ident[:, :])
                else:
                    r = mm(ps[:, 6, :], w3c[:, n - 2, :], operand[:, q, XS, :], start=True, stop=True)
                r.then_inc(s_aux, 1)

            def replicate(k, q, c, u):
                if u == 0:
                    pe.wait_ge(s_etl[q], (c + 1) * 16)
                if after(k, 1) or u >= 2:
                    pe.wait_ge(s_prod, k * STEPS + u - 1)
                for j in range(2):
                    r = {ES64A: j, ES64B: 2 + j, ES32: 4 + j}.get(u, 6 + 2 * (u - EV0) + j)
                    last = mm(ps[:, 2 * (u % 2) + j, :], rep[:, r, :], et[:, q, :], start=True, stop=True)
                last.then_inc(s_rep, 1)

            tp_s, tp_s2 = ps[0:S0, 4, :], ps[S0:P, 5, :]
            tp_v = [ps[S0:S0 + V0, 4, :], ps[S0 + V0:P, 4, :], ps[0:V0, 5, :]]

            def contract(k, u):
                pe.wait_ge(s_prod, k * STEPS + u + 1)
                if u == 0 and after(k, 1):
                    pe.wait_ge(s_tp, k)
                f = FIRST[u]
                if u in (ES64A, ES64B):
                    c = 0 if u == ES64A else 2
                    mm(tp_s, w1c[:, c, :], prod[:, f, :], start=(u == ES64A), stop=False)
                    last = mm(tp_s2, w1c[:, c + 1, :], prod[:, f + 1, :], start=(u == ES64A), stop=False)
                elif u == ES32:
                    for j in range(2):
                        for i3 in range(3):
                            last = mm(tp_v[i3], w4c[:, j, :], prod[:, f + 3 * j + i3, :], start=(j == 0), stop=False)
                else:
                    i3 = u - EV0
                    for j in range(2):
                        mm(tp_s2 if i3 == 2 else tp_s, w2c[:, j, :], prod[:, f + j, :], start=False,
                           stop=(j == 1 and i3 > 0))
                        last = mm(tp_v[i3], sum_b[:, :], prod[:, f + 2 + j, :], start=False, stop=(j == 1))
                last.then_inc(s_contr, 1)

            def source_row(k, q):
                pe.wait_ge(s_mslot, k + 1)
                if after(k, 1):
                    pe.wait_ge(s_mdc, (k - 1) * 4 + 4)
                for t in range(G):
                    for n in range(2):
                        r = mm(ps[:, 7, P * t:P * (t + 1)], srcb_slot[:, q, n, t:t + 1].to_broadcast([P, P]),
                               ident_b[:, :], start=(n == 0), stop=(n == 1))
                r.then_inc(s_row, 1)

            def messages(k, n):
                if n == 0:
                    pe.wait_ge(s_same, k + 1)
                    pe.wait_ge(s_tp, k + 1)
                else:
                    pe.wait_ge(s_mdc, k * 4 + n)
                for t in (2 * (n % 2), 2 * (n % 2) + 1):
                    o = ps[:, 7, D * (t % 2):D * (t % 2 + 1)]
                    if n < 2:
                        mm(o, tpa[:, P * t:P * (t + 1)], wfa[:, :], start=True, stop=False)
                        r = mm(o, tpb[:, P * t:P * (t + 1)], wfb[:, :], start=False, stop=True)
                    else:
                        r = mm(o, same[:, t, :], m_s[:, t, :], start=True, stop=True)
                r.then_inc(s_md, 1)

            def edge_block(k, q, c, nxt=True):
                o = 1 - q
                prev = after(k, 1)
                for u in range(STEPS):
                    replicate(k, q, c, u)
                    if u > 0:
                        contract(k, u - 1)
                    elif prev:
                        contract(k - 1, STEPS - 1)
                    if nxt and u in AUX_STEP:
                        aux(k + 1, o, c + q, AUX_STEP[u])
                    if prev and u == 0:
                        source_row(k - 1, o)
                    if prev and u >= 2:
                        messages(k - 1, u - 2)

            for n in range(AUX):
                aux(0, 0, 0, n)
            edge_block(0, 0, 0)
            edge_block(1, 1, 0)
            with pe.Fori(1, NB // 2 - 1) as i:
                for q in range(2):
                    edge_block(i * 2 + q, q, i)
            edge_block(NB - 2, 0, NB // 2 - 1)
            edge_block(NB - 1, 1, NB // 2 - 1, nxt=False)
            contract(NB - 1, STEPS - 1)
            source_row(NB - 1, 1)
            for n in range(4):
                messages(NB - 1, n)


_INS = ["x", "src", "dst", "edge_attr_32", "L0_gnn_W1", "L0_gnn_W2", "L0_gnn_W3", "L0_gnn_W4", "L0_gnn_Wm",
        "L0_gnn_bm", "L0_gnn_Wu", "L0_gnn_bu"]


def kernel(**inputs):
    import numpy as np
    import concourse.bacc as bacc
    from concourse.bass_utils import run_bass_kernel_spmd

    nc = bacc.Bacc("TRN2", target_bir_lowering=False, num_devices=1)
    arrays, args = {}, []
    for name in _INS:
        a = np.ascontiguousarray(inputs[name])
        arrays[f"in_{name}"] = a
        args.append(nc.dram_tensor(f"in_{name}", a.shape, mybir.dt.from_np(a.dtype), kind="ExternalInput").ap())
    out = nc.dram_tensor("out_rows", (NPAD, D), F32, kind="ExternalOutput").ap()
    tp_message_passing(nc, *args, out)
    r = run_bass_kernel_spmd(nc, [arrays], core_ids=[0])
    return r.results[0]["out_rows"][0:N]
```

```python
import concourse.bass as bass
from concourse import mybir
from contextlib import ExitStack

F32 = mybir.dt.float32
BF16 = mybir.dt.bfloat16
I32 = mybir.dt.int32
ALU = mybir.AluOpType
ACT = mybir.ActivationFunctionType

N = 50000
S0, V0 = 64, 32
D = S0 + 3 * V0
EB = 8
DE = EB + 3 * EB
EPS = 1e-5

P = 128
G = 4
T = -(-N // (P * G)) * G
NB = T // G
NPAD = P * T
TAIL = N - (P - 1) * T
B_FULL = TAIL // G
SPLIT = 112
W = G * P
DUMP = N
assert TAIL % G == 0 and NPAD >= N + P

RING = 7
UNROLL = 2 * RING
assert NB % UNROLL == 0

STEPS = 7
ES_A, ES_B, ES_C, OWNERS, EV0, EV1, EV2 = range(STEPS)
REPS = {ES_A: (0, 1), ES_B: (2, 4), ES_C: (3, 5), EV0: (6, 7), EV1: (8, 9), EV2: (10, 11)}
CHUNKS = {ES_A: 2, ES_B: 4, ES_C: 4, OWNERS: 0, EV0: 4, EV1: 4, EV2: 4}
FIRST = [sum(CHUNKS[v] for v in range(u)) for u in range(STEPS)]
PRODUCTS = sum(CHUNKS.values())

XS, XV, Y3 = 0, 1, 4
OPERANDS = 6
AUX_STEP = {0: 0, 4: 1, 5: 2, 6: 3}
MD_STEP = {2: 0, 4: 1, 5: 2, 6: 3}
AUX = 4


def nothing(b):
    pass


class At:

    def __init__(self, i, u):
        self.g = i * UNROLL + u
        self.slot = u % RING
        self.par = u % 2
        self.turn = i * (UNROLL // RING) + u // RING


def after(k, n):
    return not isinstance(k, int) or k >= n


def pass_over_nodes(engine, *stages):
    for u in range(UNROLL):
        for j, stage in enumerate(stages[:u + 1]):
            stage(At(0, u - j))
    with engine.Fori(1, NB // UNROLL) as i:
        for u in range(UNROLL):
            for j, stage in enumerate(stages):
                stage(At(i, u - j))
    for u in range(len(stages) - 1):
        for j, stage in enumerate(stages):
            if j > u:
                stage(At(NB // UNROLL - 1, UNROLL + u - j))


def tp_message_passing(nc, x, src, dst, e, w1, w2, w3, w4, wm, bm, wu, bu, out):
    ctx = ExitStack()
    with ctx:
        def sb(name, shape, dt):
            return ctx.enter_context(nc.sbuf_tensor(name, shape, dt))

        def sem(name):
            return ctx.enter_context(nc.semaphore(name))

        h_dram = nc.dram_tensor("h_dram", (NPAD, D), F32, kind="Internal").ap()
        et_dram = nc.dram_tensor("et_dram", (NB * 3 * DE, W), BF16, kind="Internal").ap()

        ident = sb("ident", [P, P], F32)
        ident_b = sb("ident_b", [P, P], BF16)
        upto = sb("upto", [P, P], F32)
        pick = sb("pick", [3 * DE, DE], BF16)
        rep = sb("rep", [3 * DE, 12, P], BF16)
        sum_b = sb("sum_b", [P, V0], F32)
        dump_row = sb("dump_row", [P, 1], F32)
        w1c = sb("w1c", [P, 4, S0], F32)
        w2c = sb("w2c", [P, 2, S0], F32)
        w4c = sb("w4c", [P, 2, V0], F32)
        w3c = sb("w3c", [P, 2, P], F32)
        wma = sb("wma", [P, D], F32)
        wmb = sb("wmb", [P, D], F32)
        wmta = sb("wmta", [P, 2, P], F32)
        wmtb = sb("wmtb", [P, 2, P], F32)
        wub = sb("wub", [P, 2, D], F32)
        wfa = sb("wfa", [P, D], F32)
        wfb = sb("wfb", [P, D], F32)
        wta = sb("wta", [P, D], F32)
        wtb = sb("wtb", [P, D], F32)
        perm_a = sb("perm_a", [P, D], F32)
        perm_b = sb("perm_b", [V0, D], F32)

        src_i = sb("src_i", [P, NB, G], I32)
        dst_i = sb("dst_i", [P, NB, G], I32)
        part_i = sb("part_i", [P, 2, NB, G], I32)
        src_f = sb("src_f", [P, NB, 2, G], F32)
        src_b = sb("src_b", [P, NB, 2, G], BF16)

        prod = sb("prod", [P, 2, PRODUCTS, W], F32)
        prod_flat = prod[:, :, :, :].rearrange("p a b c -> p (a b c)")
        ring_cols = RING * G * D
        x_s, h_s = (prod_flat[:, n * ring_cols:(n + 1) * ring_cols].rearrange("p (r g d) -> p r g d", r=RING, g=G)
                    for n in range(2))
        z_s = sb("z_s", [P, 2, G, D], F32)
        base_s = sb("base_s", [P, RING, G, D], F32)
        e_s = sb("e_s", [P, RING, G, DE], F32)
        ep_s = sb("ep_s", [P, 2, G, 3, DE], BF16)
        er_s = sb("er_s", [P, 2, G, DE], F32)
        et_w = sb("et_w", [3 * DE, RING, W], BF16)
        stats = sb("stats", [P, 2, G, 6], F32)
        mv = sb("mv", [P, 2, G, 2], F32)
        std = sb("std", [P, 2, G], F32)
        rstd = sb("rstd", [P, 2, G], F32)
        eps = sb("eps", [P, 1], F32)
        hta = sb("hta", [P, 2, W], F32)
        htb = sb("htb", [P, 2, W], F32)

        et = sb("et", [3 * DE, 2, W], BF16)
        hg = sb("hg", [P, 2, G, D], F32)
        operand = sb("operand", [P, 2, OPERANDS, W], F32)
        tpa = sb("tpa", [P, W], F32)
        tpb = sb("tpb", [P, W], F32)
        same = sb("same", [P, 2, G, P], F32)
        count = sb("count", [P, G], F32)
        shift = sb("shift", [P, G], F32)
        row_f = sb("row_f", [P, 2, G], F32)
        m_s = sb("m_s", [P, G, D], F32)
        dd_s = sb("dd_s", [P, 2, G, D], F32)
        dst_slot = sb("dst_slot", [P, 2, G], I32)
        srcf_slot = sb("srcf_slot", [P, 2, 2, G], F32)
        srcb_slot = sb("srcb_slot", [P, 2, 2, G], BF16)
        row_slot = sb("row_slot", [P, 2, G], I32)

        ps = ctx.enter_context(nc.psum_tensor("ps", [P, 8, W], F32))
        def pair_of(q, u):
            n = 2 * ((q * STEPS + u) % 2)
            return ps[:, n:n + 2, :]

        n_et = ps[0:3 * DE, 7, 0:W // 2].bitcast(BF16)

        s_wload = sem("weights_loaded")
        s_iload = sem("indices_loaded")
        s_const = sem("pool_constants")
        s_prep = sem("vector_prep")
        s_wt_ps = sem("weights_transposed")
        s_wt_sb = sem("weights_copied")
        s_tables = sem("tables_ready")
        s_passed = sem("pool_waits_passed")
        s_passed_v = sem("vector_waits_passed")
        s_x = [sem(f"x_loaded{q}") for q in range(RING)]
        s_e = [sem(f"e_loaded{q}") for q in range(RING)]
        s_stat = sem("node_stats")
        s_var = sem("node_variance")
        s_std = sem("node_deviation")
        s_rstd = sem("node_inverse_deviation")
        s_z = sem("node_normalised")
        s_h = sem("node_relu")
        s_ht_ps = sem("node_transposed")
        s_ht = sem("node_transposed_copied")
        s_base_ps = sem("node_product")
        s_base = sem("node_base")
        s_split = sem("edge_split_chain")
        s_ep = sem("edge_split")
        s_et_ps = sem("edge_transposed")
        s_et = sem("edge_transposed_copied")
        s_hst = [sem(f"h_stored{q}") for q in range(RING)]
        s_bst = [sem(f"base_stored{q}") for q in range(RING)]
        s_est = [sem(f"et_stored{q}") for q in range(RING)]
        s_etl = [sem(f"et_loaded{q}") for q in range(2)]
        s_dslot = sem("dst_slot_ready")
        s_mslot = sem("src_slots_ready")
        s_gath = [sem(f"h_gathered{q}") for q in range(2)]
        s_rep = sem("edge_replicated")
        s_prod = sem("products_ready")
        s_contr = sem("products_contracted")
        s_aux = sem("aux_in_psum")
        s_auxc = sem("aux_copied")
        s_tp = sem("tensor_product_copied")
        s_md = sem("messages_in_psum")
        s_mdc = sem("messages_copied")
        s_shift = sem("vector_row_shift")
        s_same = sem("same_source_ready")
        s_rows = sem("row_numbers_ready")
        s_scat = sem("scattered")

        def rows(ap, p0, p1, width, g):
            return ap.rearrange("(p t) c -> p (t c)", t=T)[p0:p1, bass.ds(g * (G * width), G * width)]

        x_head = x[0:(P - 1) * T, :]
        e_head = e[0:(P - 1) * T, :]

        def tail_rows(ap, width, g):
            return ap[(P - 1) * T:N, :].rearrange("(p t) c -> p (t c)", p=1)[:, bass.ds(g * (G * width), G * width)]

        N_WLOAD = [0]

        block = ctx.enter_context(nc.Block())

        @block.sync
        def _(sp):
            for table, flat in ((src_i, src), (dst_i, dst)):
                if table is src_i:
                    sp.wait_ge(s_prep, 2)
                v = table[:, :, :].rearrange("p b g -> p (b g)")
                head = flat[0:(P - 1) * T].rearrange("(p t) -> p t", t=T)
                sp.dma_start(v[0:SPLIT, :], head[0:SPLIT, :]).then_inc(s_iload, 16)
                sp.dma_start(v[SPLIT:P - 1, :], head[SPLIT:P - 1, :]).then_inc(s_iload, 16)
                sp.dma_start(v[P - 1:P, 0:TAIL], flat[(P - 1) * T:N].rearrange("(p t) -> p t", p=1)).then_inc(s_iload, 16)

            def load(g, q, full):
                for dst_t, head, whole, width, s in ((x_s, x_head, x, D, s_x), (e_s, e_head, e, DE, s_e)):
                    d = dst_t[:, q].rearrange("p g c -> p (g c)")
                    sp.dma_start(d[0:SPLIT, :], rows(head, 0, SPLIT, width, g)).then_inc(s[q], 16)
                    sp.dma_start(d[SPLIT:P - 1, :], rows(head, SPLIT, P - 1, width, g)).then_inc(s[q], 16)
                    if full:
                        sp.dma_start(d[P - 1:P, :], tail_rows(whole, width, g)).then_inc(s[q], 16)
                    else:
                        sp.sem_inc(s[q], 16)

            def store(g, q):
                sp.wait_ge(s_h, g + 1)
                sp.dma_start(rows(h_dram, 0, P, D, g), h_s[:, q].rearrange("p g c -> p (g c)")).then_inc(s_hst[q], 16)
                sp.wait_ge(s_et, g + 1)
                sp.dma_start(et_dram[bass.ds(g * (3 * DE), 3 * DE), :], et_w[:, q, :]).then_inc(s_est[q], 16)
                sp.wait_ge(s_base, g + 1)
                sp.dma_start(rows(out, 0, P, D, g), base_s[:, q].rearrange("p g c -> p (g c)")).then_inc(s_bst[q], 16)

            AHEAD = RING - 1

            def node_block(g, q, full):
                load(g + AHEAD, (q + AHEAD) % RING, full)
                store(g, q)

            sp.wait_ge(s_prep, 4)
            for g in range(AHEAD):
                load(g, g, True)
            node_block(0, 0, True)
            with sp.Fori(0, 6) as i:
                for q in range(RING):
                    node_block(i * RING + (q + 1), (q + 1) % RING, True)
            for g in range(43, 50):
                node_block(g, g % RING, g + AHEAD < B_FULL)
            with sp.Fori(7, 13) as i:
                for q in range(RING):
                    node_block(i * RING + (q + 1), (q + 1) % RING, False)
            for g in range(NB - AHEAD, NB):
                store(g, g % RING)

            for q in range(RING):
                sp.wait_ge(s_est[q], 16 * (NB // RING))

            def load_et(k, q):
                sp.dma_start(et[:, q, :], et_dram[bass.ds(k * (3 * DE), 3 * DE), :]).then_inc(s_etl[q], 16)

            load_et(0, 0)
            load_et(1, 1)
            with sp.Fori(1, NB // 2) as i:
                for q in range(2):
                    k = i * 2 + q
                    sp.wait_ge(s_rep, (k - 2) * STEPS + STEPS)
                    load_et(k, q)

        @block.gpsimd
        def _(pool):
            pool.memset(ident[:, :], 0.0).then_inc(s_const, 1)
            pool.memset(ident_b[:, :], 0.0).then_inc(s_const, 1)
            pool.memset(pick[:, :], 0.0).then_inc(s_const, 1)
            pool.memset(sum_b[:, :], 0.0).then_inc(s_const, 1)
            pool.memset(upto[:, :], 1.0).then_inc(s_const, 1)
            pool.iota(dump_row[:, :], [[0, 1]], base=DUMP, channel_multiplier=1,
                      allow_small_or_imprecise_dtypes=True).then_inc(s_const, 1)
            pool.wait_ge(s_const, 6)
            for m in (ident, ident_b):
                pool.affine_select(out=m[:, :], in_=m[:, :], compare_op=ALU.not_equal, fill=1.0, base=0,
                                   pattern=[[-1, P]], channel_multiplier=1).then_inc(s_const, 1)
            pool.affine_select(out=upto[:, :], in_=upto[:, :], compare_op=ALU.is_ge, fill=0.0, base=0,
                               pattern=[[-1, P]], channel_multiplier=1).then_inc(s_const, 1)
            for n in range(3):
                pool.affine_select(out=pick[:, :], in_=pick[:, :], compare_op=ALU.not_equal, fill=1.0, base=-DE * n,
                                   pattern=[[-1, DE]], channel_multiplier=1).then_inc(s_const, 1)
                pool.wait_ge(s_const, 10 + n)
            for n in range(4):
                pool.affine_select(out=sum_b[:, :], in_=sum_b[:, :], compare_op=ALU.not_equal, fill=1.0, base=-V0 * n,
                                   pattern=[[-1, V0]], channel_multiplier=1).then_inc(s_const, 1)
                pool.wait_ge(s_const, 13 + n)

            def wait(s, value):
                pool.wait_ge(s, value)
                pool.sem_inc(s_passed, 1)

            def split(b):
                def link(ins, n):
                    ins.then_inc(s_split, 1)
                    wait(s_split, b.g * 4 + n)
                wait(s_e[b.slot], (b.turn + 1) * 48)
                if after(b.g, 2):
                    wait(s_et_ps, b.g - 1)
                part, rest, e_in = ep_s[:, b.par], er_s[:, b.par], e_s[:, b.slot]
                link(pool.tensor_copy(part[:, :, 0, :], e_in), 1)
                link(pool.tensor_tensor(rest, e_in, part[:, :, 0, :], ALU.subtract), 2)
                link(pool.tensor_copy(part[:, :, 1, :], rest), 3)
                link(pool.tensor_tensor(rest, rest, part[:, :, 1, :], ALU.subtract), 4)
                pool.tensor_copy(part[:, :, 2, :], rest).then_inc(s_ep, 1)

            pass_over_nodes(pool, split)

            def gather(k, q, t):
                pool.indirect_dma_start(
                    out=hg[:, q, t, :], out_offset=None, in_=h_dram,
                    in_offset=bass.IndirectOffsetOnAxis(ap=dst_slot[:, q, t:t + 1], axis=0),
                ).then_inc(s_gath[q], 16)

            def scatter(k, q, t):
                if t in (0, 2):
                    wait(s_mdc, k * 4 + 3 + t // 2)
                if after(k, 1) or t > 0:
                    wait(s_scat, k * (G * 16) + t * 16)
                pool.indirect_dma_start(
                    out=out, out_offset=bass.IndirectOffsetOnAxis(ap=row_slot[:, q, t:t + 1], axis=0),
                    in_=dd_s[:, q, t, :], in_offset=None, compute_op=ALU.add,
                ).then_inc(s_scat, 16)

            for q in range(RING):
                pool.wait_ge(s_hst[q], 16 * (NB // RING))
            for k in range(2):
                wait(s_dslot, k + 1)
                for t in range(G):
                    gather(k, k, t)
            for q in range(RING):
                pool.wait_ge(s_bst[q], 16 * (NB // RING))

            def edge_block(k, q, with_gather=True):
                if with_gather:
                    wait(s_aux, k * AUX + 2)
                    wait(s_dslot, k + 3)
                if after(k, 2):
                    wait(s_rows, k - 1)
                for t in range(G):
                    if with_gather:
                        gather(k + 2, q, t)
                    if after(k, 2):
                        scatter(k - 2, q, t)

            for k in range(4):
                edge_block(k, k % 2)
            with pool.Fori(2, NB // 2 - 1) as i:
                for q in range(2):
                    edge_block(i * 2 + q, q)
            for k in range(NB - 2, NB + 2):
                edge_block(k, k % 2, with_gather=False)
            pool.wait_ge(s_scat, NB * G * 16)

        @block.scalar
        def _(act):
            def ld(dst_ap, src_ap):
                act.dma_start(dst_ap, src_ap).then_inc(s_wload, 16)
                N_WLOAD[0] += 16

            act.wait_ge(s_prep, 1)
            for b in range(EB):
                ld(w1c[S0 * (b % 2):S0 * (b % 2 + 1), b // 2, :], w1[:, b, :])
                ld(w2c[V0 * (b % 4):V0 * (b % 4 + 1), b // 4, :], w2[:, b, :])
                ld(w4c[V0 * (b % 4):V0 * (b % 4 + 1), b // 4, :], w4[:, b, :])
            ld(w3c[0:S0, :, :], w3.rearrange("a (j b) c -> a j (b c)", j=2))

            def in_order(dst_a, dst_b, mat):
                vec = mat[S0:D, :].rearrange("(c i) n -> c i n", i=3)
                ld(dst_a[0:S0, :], mat[0:S0, :])
                ld(dst_a[S0:S0 + V0, :], vec[:, 0, :])
                ld(dst_a[S0 + V0:P, :], vec[:, 1, :])
                ld(dst_b[0:V0, :], vec[:, 2, :])

            in_order(wma, wmb, wm)
            ld(wmb[V0:V0 + 1, :], bm.rearrange("(o n) -> o n", o=1))
            ld(wmb[S0:P, :], wm[0:S0, :])
            in_order(wta, wtb, wu[0:D, :])
            ld(wtb[V0:V0 + 1, :], bu.rearrange("(o n) -> o n", o=1))
            ld(wub[:, 0, :], wu[D:D + P, :])
            ld(wub[0:D - P, 1, :], wu[D + P:2 * D, :])

            act.wait_ge(s_wt_ps, 1)
            nc.scalar.activation(wmta[:, :, :], ps[:, 0, 0:2 * P].rearrange("p (a b) -> p a b", a=2), ACT.Copy)
            nc.scalar.activation(wmtb[0:V0, :, :], ps[0:V0, 1, 0:2 * P].rearrange("p (a b) -> p a b", a=2),
                                 ACT.Copy).then_inc(s_wt_sb, 1)
            act.wait_ge(s_wt_ps, 2)
            nc.scalar.activation(wfa[:, :], ps[:, 2, 0:D], ACT.Copy)
            nc.scalar.activation(wfb[:, :], ps[:, 3, 0:D], ACT.Copy).then_inc(s_wt_sb, 1)

            def deviation(b):
                act.wait_ge(s_var, b.g + 1)
                if after(b.g, 2):
                    act.wait_ge(s_rstd, b.g - 1)
                nc.scalar.activation(std[:, b.par, :], mv[:, b.par, :, 1], ACT.Sqrt, bias=eps[:, 0:1],
                                     scale=1.0).then_inc(s_std, 1)

            def relu(b):
                act.wait_ge(s_z, b.g + 1)
                if after(b.g, RING):
                    act.wait_ge(s_hst[b.slot], b.turn * 16)
                nc.scalar.activation(h_s[:, b.slot, :, 0:S0], z_s[:, b.par, :, 0:S0], ACT.Relu)
                nc.scalar.activation(h_s[:, b.slot, :, S0:D].rearrange("p g (i c) -> p g i c", i=3),
                                     z_s[:, b.par, :, S0:D].rearrange("p g (c i) -> p g i c", i=3),
                                     ACT.Relu).then_inc(s_h, 1)

            def copy_transposed(b):
                act.wait_ge(s_ht_ps, b.g + 1)
                if after(b.g, 2):
                    act.wait_ge(s_base_ps, b.g - 1)
                nc.scalar.activation(hta[:, b.par, :], ps[:, b.par, :], ACT.Copy)
                nc.scalar.activation(htb[0:V0, b.par, :], ps[0:V0, 2, :], ACT.Copy).then_inc(s_ht, 1)
                act.wait_ge(s_et_ps, b.g + 1)
                if after(b.g, RING):
                    act.wait_ge(s_est[b.slot], b.turn * 16)
                nc.scalar.activation(et_w[:, b.slot, :], n_et, ACT.Copy).then_inc(s_et, 1)

            pass_over_nodes(act, deviation, relu, copy_transposed)

            act.wait_ge(s_tables, 1)

            def slot_dst(k, q):
                nc.scalar.activation(dst_slot[:, q, :], dst_i[:, bass.ds(k, 1), :].rearrange("p b g -> p (b g)"),
                                     ACT.Copy).then_inc(s_dslot, 1)

            def slot_src(k, q):
                nc.scalar.activation(srcf_slot[:, q].rearrange("p a g -> p (a g)"),
                                     src_f[:, bass.ds(k, 1)].rearrange("p b a g -> p (b a g)"), ACT.Copy)
                nc.scalar.activation(srcb_slot[:, q].rearrange("p a g -> p (a g)"),
                                     src_b[:, bass.ds(k, 1)].rearrange("p b a g -> p (b a g)"), ACT.Copy).then_inc(s_mslot, 1)

            def copy_aux(k, q, n):
                act.wait_ge(s_aux, k * AUX + n + 1)
                if n == 0:
                    for r in range(2):
                        last = nc.scalar.activation(operand[S0 * r:S0 * (r + 1), q, XS, :], ps[0:S0, 6, :], ACT.Copy)
                    for i3 in range(2):
                        for r in range(4):
                            last = nc.scalar.activation(operand[V0 * r:V0 * (r + 1), q, XV + i3, :],
                                                        ps[S0 + V0 * i3:S0 + V0 * (i3 + 1), 6, :], ACT.Copy)
                elif n == 1:
                    for r in range(4):
                        last = nc.scalar.activation(operand[V0 * r:V0 * (r + 1), q, XV + 2, :], ps[0:V0, 6, :], ACT.Copy)
                else:
                    last = nc.scalar.activation(operand[:, q, Y3 + n - 2, :], ps[:, 6, :], ACT.Copy)
                last.then_inc(s_auxc, 1)

            def copy_md(k, q, n):
                act.wait_ge(s_md, k * 4 + n + 1)
                if n == 2 and after(k, 2):
                    act.wait_ge(s_scat, (k - 1) * (G * 16))
                j = n % 2
                dest = m_s[:, 2 * j:2 * j + 2, :] if n < 2 else dd_s[:, q, 2 * j:2 * j + 2, :]
                nc.scalar.activation(dest, ps[:, 7, 0:2 * D].rearrange("p (a b) -> p a b", a=2), ACT.Copy).then_inc(s_mdc, 1)

            def copy_tp(k):
                act.wait_ge(s_contr, k + 1)
                if after(k, 1):
                    act.wait_ge(s_md, (k - 1) * 4 + 2)
                nc.scalar.activation(tpa[:, :], ps[:, 4, :], ACT.Copy)
                nc.scalar.activation(tpb[0:V0, :], ps[0:V0, 5, :], ACT.Copy)
                nc.scalar.activation(tpb[S0:P, :], ps[S0:P, 5, :], ACT.Copy).then_inc(s_tp, 1)

            def edge_block(k, q, nxt=True, nxt2=True):
                o = 1 - q
                prev = after(k, 1)
                if prev:
                    copy_tp(k - 1)
                if nxt:
                    if prev:
                        act.wait_ge(s_same, k)
                    slot_src(k + 1, o)
                if nxt2:
                    act.wait_ge(s_aux, k * AUX + 2)
                    slot_dst(k + 2, q)
                if nxt and prev:
                    act.wait_ge(s_prod, k * STEPS)
                for n in range(4):
                    if nxt:
                        copy_aux(k + 1, o, n)
                    if prev:
                        copy_md(k - 1, o, n)

            slot_dst(0, 0)
            slot_dst(1, 1)
            slot_src(0, 0)
            for n in range(AUX):
                copy_aux(0, 0, n)
            for k in range(4):
                edge_block(k, k % 2)
            with act.Fori(2, NB // 2 - 1) as i:
                for q in range(2):
                    edge_block(i * 2 + q, q)
            edge_block(NB - 2, 0, nxt2=False)
            edge_block(NB - 1, 1, nxt=False, nxt2=False)
            copy_tp(NB - 1)
            for n in range(4):
                copy_md(NB - 1, 1, n)

        @block.vector
        def _(dve):
            v = nc.vector
            for m in (w3c[:, :, :], wmb[:, :], wub[:, :, :], wtb[:, :], wmtb[:, :, :]):
                last = v.memset(m, 0.0)
            last.then_inc(s_prep, 1)
            v.memset(dst_i[:, :, :], 0)
            v.memset(eps[:, :], EPS)
            v.memset(tpb[:, :], 0.0)
            dve.wait_ge(s_const, 6)
            v.tensor_scalar(src_i[:, :, :].rearrange("p b g -> p (b g)"),
                            dump_row[:, 0:1].to_broadcast([P, T]), 0.0, None, ALU.add).then_inc(s_prep, 1)
            v.memset(htb[:, :, :], 0.0).then_inc(s_prep, 1)
            v.memset(x_s[:, :, :, :], 0.0)
            v.memset(e_s[:, :, :, :], 0.0).then_inc(s_prep, 1)
            dve.wait_ge(s_prep, 4)
            v.memset(tpb[V0:V0 + 1, :], 1.0)
            v.memset(htb[V0:V0 + 1, :, :], 1.0).then_inc(s_prep, 1)

            dve.wait_ge(s_const, 12)
            for r in range(12):
                if r < 4:
                    cols, n = pick[:, 2 * r:2 * r + 2], S0
                elif r < 6:
                    cols, n = pick[:, 4 * (r - 4):4 * (r - 4) + 4], V0
                else:
                    i3, j = (r - 6) // 2, (r - 6) % 2
                    cols, n = pick[:, EB:DE].rearrange("k (b i) -> k i b", i=3)[:, i3, 4 * j:4 * j + 4], V0
                v.tensor_copy(rep[:, r, :].rearrange("k (b a) -> k b a", a=n),
                              cols[:, :, None].to_broadcast([3 * DE, P // n, n]))

            dve.wait_ge(s_wload, N_WLOAD[0])
            half = 0.5 ** 0.5
            for m, scale in ((w1c, (S0 * EB) ** -0.5 * half), (w2c, (3.0 * V0 * EB) ** -0.5 * half),
                             (w4c, (V0 * EB) ** -0.5 * half), (w3c, (S0 * EB) ** -0.5 * half)):
                v.tensor_scalar(m[:, :, :], m[:, :, :], scale, None, ALU.mult)
            v.memset(perm_a[:, :], 0.0)
            v.memset(perm_b[:, :], 0.0).then_inc(s_prep, 1)
            dve.wait_ge(s_prep, 6)
            dve.wait_ge(s_const, 9)
            v.tensor_copy(perm_a[0:S0, 0:S0], ident[0:S0, 0:S0])
            for i3, (m, r0) in enumerate(((perm_a, S0), (perm_a, S0 + V0), (perm_b, 0))):
                last = v.tensor_copy(m[r0:r0 + V0, S0:D].rearrange("r (c i) -> r i c", i=3)[:, i3, :],
                                     ident[r0:r0 + V0, r0:r0 + V0])
            last.then_inc(s_prep, 1)
            dve.wait_ge(s_prep, 7)
            v.tensor_tensor(wta[:, :], wta[:, :], perm_a[:, :], ALU.add)
            v.tensor_tensor(wtb[0:V0, :], wtb[0:V0, :], perm_b[:, :], ALU.add).then_inc(s_prep, 1)

            dve.wait_ge(s_iload, 96)
            v.tensor_copy(src_f[:, :, 0, :], src_i[:, :, :])
            v.tensor_scalar(part_i[:, 0], src_i[:, :, :], 8, 8, ALU.logical_shift_right, ALU.logical_shift_left)
            v.tensor_scalar(part_i[:, 1], src_i[:, :, :], 255, None, ALU.bitwise_and).then_inc(s_prep, 1)
            dve.wait_ge(s_prep, 9)
            v.tensor_scalar(src_f[:, :, 1, :], src_f[:, :, 0, :], -1.0, dump_row[:, 0:1], ALU.mult, ALU.add)
            v.tensor_copy(src_b[:, :, 0, :], part_i[:, 0])
            v.tensor_copy(src_b[:, :, 1, :], part_i[:, 1]).then_inc(s_tables, 1)

            def statistics(b):
                dve.wait_ge(s_x[b.slot], (b.turn + 1) * 48)
                for t in range(G):
                    last = v.bn_stats(out=stats[:, b.par, t, :], in_=x_s[:, b.slot, t, :])
                last.then_inc(s_stat, 1)
                dve.wait_ge(s_stat, b.g + 1)
                dve.sem_inc(s_passed_v, 1)
                for t in range(G):
                    last = v.bn_aggr(out=mv[:, b.par, t, :], in_=stats[:, b.par, t, :])
                last.then_inc(s_var, 1)

            def normalise(b):
                dve.wait_ge(s_std, b.g + 1)
                v.reciprocal(rstd[:, b.par, :], std[:, b.par, :]).then_inc(s_rstd, 1)
                dve.wait_ge(s_rstd, b.g + 1)
                if after(b.g, 2):
                    dve.wait_ge(s_h, b.g - 1)
                for t in range(G):
                    last = v.tensor_scalar(z_s[:, b.par, t, :], x_s[:, b.slot, t, :], mv[:, b.par, t, 0:1],
                                           rstd[:, b.par, t:t + 1], ALU.subtract, ALU.mult)
                last.then_inc(s_z, 1)

            def add_base(b):
                dve.wait_ge(s_base_ps, b.g + 1)
                if after(b.g, RING):
                    dve.wait_ge(s_bst[b.slot], b.turn * 16)
                for j in range(2):
                    last = v.tensor_tensor(base_s[:, b.slot, 2 * j:2 * j + 2, :],
                                           ps[:, 3 + 2 * b.par + j, 0:2 * D].rearrange("p (a b) -> p a b", a=2),
                                           x_s[:, b.slot, 2 * j:2 * j + 2, :], ALU.add)
                last.then_inc(s_base, 1)

            pass_over_nodes(dve, statistics, normalise, nothing, add_base)

            def products(k, q, u):
                dve.wait_ge(s_rep, k * STEPS + u + 1)
                if u == 0:
                    dve.wait_ge(s_auxc, (k + 1) * AUX)
                    if after(k, 2):
                        dve.wait_ge(s_contr, k - 1)
                pair = pair_of(q, u)
                op = operand[:, q]
                f = FIRST[u]
                if u == ES_A:
                    last = v.tensor_tensor(prod[:, q, f:f + 2, :], op[:, XS:XS + 1, :].to_broadcast([P, 2, W]), pair, ALU.mult)
                elif u in (ES_B, ES_C):
                    v.tensor_tensor(prod[:, q, f, :], op[:, XS, :], pair[:, 0, :], ALU.mult)
                    last = v.tensor_tensor(prod[:, q, f + 1:f + 4, :], op[:, XV:XV + 3, :],
                                           pair[:, 1:2, :].to_broadcast([P, 3, W]), ALU.mult)
                else:
                    i3 = u - EV0
                    v.tensor_tensor(prod[:, q, f:f + 2, :], op[:, XV + i3:XV + i3 + 1, :].to_broadcast([P, 2, W]),
                                    pair, ALU.mult)
                    last = v.tensor_tensor(prod[:, q, f + 2:f + 4, :], op[:, Y3:Y3 + 2, :], pair, ALU.mult)
                last.then_inc(s_prod, 1)

            def owners(k, q):
                dve.wait_ge(s_rep, k * STEPS + OWNERS + 1)
                dve.wait_ge(s_mslot, k + 1)
                if after(k, 2):
                    dve.wait_ge(s_md, (k - 2) * 4 + 4)
                for t in range(G):
                    last = v.scalar_tensor_tensor(out=same[:, q, t, :], in0=pair_of(q, OWNERS)[:, 0, P * t:P * (t + 1)],
                                                  scalar=srcf_slot[:, q, 0, t:t + 1], in1=upto[:, :],
                                                  op0=ALU.is_equal, op1=ALU.mult, accum_out=count[:, t:t + 1])
                last.then_inc(s_prod, 1)
                dve.wait_ge(s_prod, k * STEPS + OWNERS + 1)
                v.scalar_tensor_tensor(out=shift[:, :], in0=count[:, :], scalar=1.5, in1=srcf_slot[:, q, 1, :],
                                       op0=ALU.is_gt, op1=ALU.mult).then_inc(s_shift, 1)
                dve.wait_ge(s_shift, k + 1)
                v.tensor_tensor(row_f[:, q, :], shift[:, :], srcf_slot[:, q, 0, :], ALU.add).then_inc(s_same, 1)

            def row_numbers(k, q):
                dve.wait_ge(s_same, k + 1)
                if after(k, 2):
                    dve.wait_ge(s_scat, (k - 1) * (G * 16))
                v.tensor_copy(row_slot[:, q, :], row_f[:, q, :]).then_inc(s_rows, 1)

            def edge_block(k, q):
                for u in range(STEPS):
                    if u == OWNERS:
                        owners(k, q)
                    else:
                        products(k, q, u)
                    if u == EV0 and after(k, 1):
                        row_numbers(k - 1, 1 - q)

            for k in range(2):
                edge_block(k, k)
            with dve.Fori(1, NB // 2) as i:
                for q in range(2):
                    edge_block(i * 2 + q, q)
            row_numbers(NB - 1, 1)

        @block.tensor
        def _(pe):
            mm = nc.tensor.matmul
            pe.wait_ge(s_wload, N_WLOAD[0])
            pe.wait_ge(s_const, 16)
            for n, m in enumerate((wma, wmb)):
                nc.tensor.transpose(ps[:, 0, P * n:P * (n + 1)], m[:, 0:P], ident[:, :])
                last = nc.tensor.transpose(ps[0:D - P, 1, P * n:P * (n + 1)], m[:, P:D], ident[:, :])
            last.then_inc(s_wt_ps, 1)
            pe.wait_ge(s_wt_sb, 1)
            for n in range(2):
                mm(ps[:, 2 + n, 0:D], wmta[:, n, :], wub[:, 0, :], start=True, stop=False)
                last = mm(ps[:, 2 + n, 0:D], wmtb[:, n, :], wub[:, 1, :], start=False, stop=True)
            last.then_inc(s_wt_ps, 1)
            pe.wait_ge(s_wt_sb, 2)
            pe.wait_ge(s_prep, 8)

            def transposes(b):
                pe.wait_ge(s_h, b.g + 1)
                if after(b.g, 1):
                    pe.wait_ge(s_ht, b.g)
                for t in range(G):
                    nc.tensor.transpose(ps[:, b.par, P * t:P * (t + 1)], h_s[:, b.slot, t, 0:P], ident[:, :])
                for t in range(G):
                    last = nc.tensor.transpose(ps[0:V0, 2, P * t:P * (t + 1)], h_s[:, b.slot, t, P:D], ident[:, :])
                last.then_inc(s_ht_ps, 1)
                pe.wait_ge(s_ep, b.g + 1)
                if after(b.g, 1):
                    pe.wait_ge(s_et, b.g)
                for t in range(G):
                    last = nc.tensor.transpose(n_et[:, P * t:P * (t + 1)],
                                               ep_s[:, b.par, t].rearrange("p a b -> p (a b)"), ident_b[:, :])
                last.then_inc(s_et_ps, 1)

            def product(b):
                pe.wait_ge(s_ht, b.g + 1)
                if after(b.g, 2):
                    pe.wait_ge(s_base, b.g - 1)
                for t in range(G):
                    o = ps[:, 3 + 2 * b.par + t // 2, D * (t % 2):D * (t % 2 + 1)]
                    mm(o, hta[:, b.par, P * t:P * (t + 1)], wta[:, :], start=True, stop=False)
                    last = mm(o, htb[:, b.par, P * t:P * (t + 1)], wtb[:, :], start=False, stop=True)
                last.then_inc(s_base_ps, 1)

            pass_over_nodes(pe, transposes, product)

            pe.wait_ge(s_base, NB)
            pe.wait_ge(s_et, NB)

            def aux(k, q, c, n):
                if after(k, 1) or n > 0:
                    pe.wait_ge(s_auxc, k * AUX + n)
                if n == 0:
                    pe.wait_ge(s_gath[q], (c + 1) * (G * 16))
                    for t in range(G):
                        r = nc.tensor.transpose(ps[:, 6, P * t:P * (t + 1)], hg[:, q, t, 0:P], ident[:, :])
                elif n == 1:
                    for t in range(G):
                        r = nc.tensor.transpose(ps[0:V0, 6, P * t:P * (t + 1)], hg[:, q, t, P:D], ident[:, :])
                else:
                    r = mm(ps[:, 6, :], w3c[:, n - 2, :], operand[:, q, XS, :], start=True, stop=True)
                r.then_inc(s_aux, 1)

            def replicate(k, q, c, u):
                if u == 0:
                    pe.wait_ge(s_etl[q], (c + 1) * 16)
                if u == OWNERS:
                    pe.wait_ge(s_mslot, k + 1)
                if after(k, 1) or u >= 2:
                    pe.wait_ge(s_prod, k * STEPS + u - 1)
                pair = pair_of(q, u)
                if u == OWNERS:
                    for t in range(G):
                        for n in range(2):
                            last = mm(pair[:, 0, P * t:P * (t + 1)], srcb_slot[:, q, n, t:t + 1].to_broadcast([P, P]),
                                      ident_b[:, :], start=(n == 0), stop=(n == 1))
                else:
                    for j in range(2):
                        last = mm(pair[:, j, :], rep[:, REPS[u][j], :], et[:, q, :], start=True, stop=True)
                last.then_inc(s_rep, 1)

            tp_s = [ps[0:S0, 4, :], ps[S0:P, 5, :]]
            tp_v = [ps[S0:S0 + V0, 4, :], ps[S0 + V0:P, 4, :], ps[0:V0, 5, :]]

            def contract(k, q, u):
                pe.wait_ge(s_prod, k * STEPS + u + 1)
                if u == ES_A and after(k, 1):
                    pe.wait_ge(s_tp, k)
                pr = prod[:, q]
                f = FIRST[u]
                if u == ES_A:
                    for h in range(2):
                        mm(tp_s[h], w1c[:, h, :], pr[:, f + h, :], start=True, stop=False)
                elif u == ES_B:
                    mm(tp_s[0], w1c[:, 2, :], pr[:, f, :], start=False, stop=False)
                    for i3 in range(3):
                        mm(tp_v[i3], w4c[:, 0, :], pr[:, f + 1 + i3, :], start=True, stop=False)
                elif u == ES_C:
                    mm(tp_s[1], w1c[:, 3, :], pr[:, f, :], start=False, stop=False)
                    for i3 in range(3):
                        mm(tp_v[i3], w4c[:, 1, :], pr[:, f + 1 + i3, :], start=False, stop=False)
                else:
                    for j in range(2):
                        mm(tp_s[j], w2c[:, j, :], pr[:, f + j, :], start=False, stop=(u == EV2))
                if u == EV2:
                    for j in range(2):
                        for i3 in range(3):
                            last = mm(tp_v[i3], sum_b[:, :], pr[:, FIRST[EV0 + i3] + 2 + j, :], start=False, stop=(j == 1))
                    last.then_inc(s_contr, 1)

            def messages(k, q, n):
                if n == 0:
                    pe.wait_ge(s_tp, k + 1)
                if n > 0 or after(k, 1):
                    pe.wait_ge(s_mdc, k * 4 + n)
                for t in (2 * (n % 2), 2 * (n % 2) + 1):
                    o = ps[:, 7, D * (t % 2):D * (t % 2 + 1)]
                    if n < 2:
                        mm(o, tpa[:, P * t:P * (t + 1)], wfa[:, :], start=True, stop=False)
                        last = mm(o, tpb[:, P * t:P * (t + 1)], wfb[:, :], start=False, stop=True)
                    else:
                        last = mm(o, same[:, q, t, :], m_s[:, t, :], start=True, stop=True)
                last.then_inc(s_md, 1)

            CONTRACT = {ES_A: [], ES_B: [], ES_C: [ES_A], OWNERS: [ES_B], EV0: [ES_C], EV1: [EV0], EV2: [EV1]}

            def edge_block(k, q, c, nxt=True):
                o = 1 - q
                prev = after(k, 1)
                for u in range(STEPS):
                    replicate(k, q, c, u)
                    if u == 0 and prev:
                        contract(k - 1, o, EV2)
                    for w in CONTRACT[u]:
                        contract(k, q, w)
                    if nxt and u in AUX_STEP:
                        aux(k + 1, o, c + q, AUX_STEP[u])
                    if prev and u in MD_STEP:
                        messages(k - 1, o, MD_STEP[u])

            for n in range(AUX):
                aux(0, 0, 0, n)
            edge_block(0, 0, 0)
            edge_block(1, 1, 0)
            with pe.Fori(1, NB // 2 - 1) as i:
                for q in range(2):
                    edge_block(i * 2 + q, q, i)
            edge_block(NB - 2, 0, NB // 2 - 1)
            edge_block(NB - 1, 1, NB // 2 - 1, nxt=False)
            contract(NB - 1, 1, EV2)
            for n in range(4):
                messages(NB - 1, 1, n)


_INS = ["x", "src", "dst", "edge_attr_32", "L0_gnn_W1", "L0_gnn_W2", "L0_gnn_W3", "L0_gnn_W4", "L0_gnn_Wm",
        "L0_gnn_bm", "L0_gnn_Wu", "L0_gnn_bu"]


def kernel(**inputs):
    import numpy as np
    import concourse.bacc as bacc
    from concourse.bass_utils import run_bass_kernel_spmd

    nc = bacc.Bacc("TRN2", target_bir_lowering=False, num_devices=1)
    arrays, args = {}, []
    for name in _INS:
        a = np.ascontiguousarray(inputs[name])
        arrays[f"in_{name}"] = a
        args.append(nc.dram_tensor(f"in_{name}", a.shape, mybir.dt.from_np(a.dtype), kind="ExternalInput").ap())
    out = nc.dram_tensor("out_rows", (NPAD, D), F32, kind="ExternalOutput").ap()
    tp_message_passing(nc, *args, out)
    r = run_bass_kernel_spmd(nc, [arrays], core_ids=[0])
    return r.results[0]["out_rows"][0:N]
```

```python
import concourse.bass as bass
from concourse import mybir
from contextlib import ExitStack

F32 = mybir.dt.float32
BF16 = mybir.dt.bfloat16
I32 = mybir.dt.int32
ALU = mybir.AluOpType
ACT = mybir.ActivationFunctionType

N = 50000
S0, V0 = 64, 32
D = S0 + 3 * V0
EB = 8
DE = EB + 3 * EB
EPS = 1e-5

P = 128
G = 4
T = -(-N // (P * G)) * G
NB = T // G
NPAD = P * T
TAIL = N - (P - 1) * T
SPLIT = 112

RING = 14
RING2 = RING // 2
NB2 = NB // 2
FULL2 = TAIL // (2 * G)
assert NB % RING == 0 and TAIL % (2 * G) == 0

SRC_ROW = 3 * DE
KE = 112

STEPS = 6
EV0, EV1, OWNERS, ES0, EV2, ES1 = range(STEPS)
EV = (EV0, EV1, EV2)
REPS = {ES0: (0,), ES1: (1,), OWNERS: (8,), EV0: (2, 3), EV1: (4, 5), EV2: (6, 7)}
CHUNKS = {ES0: 5, ES1: 5, OWNERS: 0, EV0: 4, EV1: 4, EV2: 4}
FIRST = [sum(CHUNKS[v] for v in range(u)) for u in range(STEPS)]
PRODUCTS = sum(CHUNKS.values())

XS, XV, Y3 = 0, 2, 5
OPERANDS = 7
V_BY_DMA = ((XV, S0),)
S_BY_DMA = ((XS, 0), (XS + 1, V0))
AUX_STEP = {1: 0, 2: 1, 3: 2, 4: 3}
AUX = 4
CONTRACT = {EV2: ES0, ES1: EV2}
ADDS = {2: ((1, 0),), 3: ((1, 1),), 4: ((2, 0), (2, 1))}
ADDS_PER_BLOCK = 4
MD_STEP = {1: (2, 3), 2: (1, 0), 3: (1, 1), 4: (1, 2)}
W = G * P
DUMP = N
assert TAIL % G == 0 and NPAD >= N + P and S0 == 2 * V0 and P == 4 * V0


class At:

    def __init__(self, i, u):
        self.g = i * RING + u
        self.slot = u % RING
        self.slot2 = self.slot // 2
        self.par = u % 2
        self.turn = i + u // RING


def after(k, n):
    return not isinstance(k, int) or k >= n


def pass_over_nodes(engine, *stages):
    for u in range(RING):
        for stage, lag in stages:
            if u >= lag:
                stage(At(0, u - lag))
    with engine.Fori(1, NB // RING) as i:
        for u in range(RING):
            for stage, lag in stages:
                stage(At(i, u - lag))
    for u in range(max(lag for _, lag in stages)):
        for stage, lag in stages:
            if u < lag:
                stage(At(NB // RING - 1, RING + u - lag))


def tp_message_passing(nc, x, src, dst, e, w1, w2, w3, w4, wm, bm, wu, bu, out):
    ctx = ExitStack()
    with ctx:
        def sb(name, shape, dt):
            return ctx.enter_context(nc.sbuf_tensor(name, shape, dt))

        def sem(name):
            return ctx.enter_context(nc.semaphore(name))

        h_dram = nc.dram_tensor("h_dram", (NPAD, D), F32, kind="Internal").ap()
        et_dram = nc.dram_tensor("et_dram", (NB * KE, W), BF16, kind="Internal").ap()

        ident = sb("ident", [P, P], F32)
        ident_b = sb("ident_b", [P, P], BF16)
        upto = sb("upto", [P, P], F32)
        pick = sb("pick", [KE, DE], BF16)
        rep = sb("rep", [KE, 9, P], BF16)
        sum_b = sb("sum_b", [P, V0], F32)
        dump_row = sb("dump_row", [P, 1], F32)
        w1c = sb("w1c", [P, 2, 2, S0], F32)
        w2c = sb("w2c", [P, 2, S0], F32)
        w4c = sb("w4c", [P, 2, V0], F32)
        w3c = sb("w3c", [P, 2, P], F32)
        wma = sb("wma", [P, D], F32)
        wmb = sb("wmb", [P, D], F32)
        wmta = sb("wmta", [P, 2, P], F32)
        wmtb = sb("wmtb", [P, 2, P], F32)
        wub = sb("wub", [P, 2, D], F32)
        wfa = sb("wfa", [P, D], F32)
        wfb = sb("wfb", [P, D], F32)
        wta = sb("wta", [P, D], F32)
        wtb = sb("wtb", [P, D], F32)
        perm_a = sb("perm_a", [P, D], F32)
        perm_b = sb("perm_b", [V0, D], F32)

        src_i = sb("src_i", [P, NB, G], I32)
        dst_i = sb("dst_i", [P, NB, G], I32)
        part_i = sb("part_i", [P, 2, NB, G], I32)
        src_f = sb("src_f", [P, NB, 2, G], F32)
        src_b = sb("src_b", [P, NB, 2, G], BF16)

        prod = sb("prod", [P, 2, PRODUCTS, W], F32)
        prod_flat = prod[:, :, :, :].rearrange("p a b c -> p (a b c)")
        ring_cols = RING * G * D
        x_s, h_s = (prod_flat[:, n * ring_cols:(n + 1) * ring_cols].rearrange("p (r g d) -> p r g d", r=RING, g=G)
                    for n in range(2))
        z_s = prod_flat[:, 2 * ring_cols:2 * ring_cols + 2 * G * D].rearrange("p (q g d) -> p q g d", q=2, g=G)
        e_at = 2 * ring_cols + 2 * G * D
        e_s = prod_flat[:, e_at:e_at + RING * G * DE].rearrange("p (r g d) -> p r g d", r=RING, g=G)
        ep_s = sb("ep_s", [P, 2, G, KE], BF16)
        er_s = sb("er_s", [P, 2, G, DE], F32)
        et_w = sb("et_w", [KE, RING, W], BF16)
        stats = sb("stats", [P, 2, G, 6], F32)
        mv = sb("mv", [P, 2, G, 2], F32)
        std = sb("std", [P, 2, G], F32)
        rstd = sb("rstd", [P, 2, G], F32)
        eps = sb("eps", [P, 1], F32)
        hta = sb("hta", [P, 2, W], F32)
        htb = sb("htb", [P, 2, W], F32)

        et = sb("et", [KE, 2, W], BF16)
        hg = sb("hg", [P, 2, G, D], F32)
        operand = sb("operand", [P, 2, OPERANDS, W], F32)
        ht_raw = sb("ht_raw", [P, W], F32)
        tp = sb("tp", [P, 2, W], F32)
        same = sb("same", [P, 2, G, P], F32)
        count = sb("count", [P, G], F32)
        shift = sb("shift", [P, G], F32)
        row_f = sb("row_f", [P, 2, G], F32)
        m_s = sb("m_s", [P, G, D], F32)
        dd_s = sb("dd_s", [P, 2, G, D], F32)
        dst_slot = sb("dst_slot", [P, 2, G], I32)
        srcf_slot = sb("srcf_slot", [P, 2, 2, G], F32)
        row_slot = sb("row_slot", [P, 2, G], I32)

        ps = ctx.enter_context(nc.psum_tensor("ps", [P, 8, W], F32))
        def pair_of(u):
            n = 2 * (u % 2)
            return ps[:, n:n + 2, :]

        n_et = ps[0:KE, 7, 0:W // 2].bitcast(BF16)

        s_wuload = sem("node_weights_loaded")
        s_wload = sem("weights_loaded")
        s_iload = sem("indices_loaded")
        s_const = sem("pool_constants")
        s_zero = sem("weights_zeroed")
        s_pad = sem("indices_padded")
        s_prep = sem("vector_prep")
        s_wt = sem("node_weights_ready")
        s_scaled = sem("tensor_product_weights_ready")
        s_wt_ps = sem("weights_transposed")
        s_wt_sb = sem("weights_copied")
        s_tables = sem("tables_ready")
        s_passed = sem("pool_waits_passed")
        s_passed_v = sem("vector_waits_passed")
        s_x = [sem(f"x_loaded{q}") for q in range(RING2)]
        s_e = [sem(f"e_loaded{q}") for q in range(RING2)]
        s_stat = sem("node_stats")
        s_var = sem("node_variance")
        s_std = sem("node_deviation")
        s_rstd = sem("node_inverse_deviation")
        s_z = sem("node_normalised")
        s_h = sem("node_relu")
        s_ht_ps = sem("node_transposed")
        s_ht = sem("node_transposed_copied")
        s_base_ps = sem("node_product")
        s_base = sem("node_base")
        s_split = sem("edge_split_chain")
        s_ep = sem("edge_split")
        s_et_ps = sem("edge_transposed")
        s_et = sem("edge_transposed_copied")
        s_hst = [sem(f"h_stored{q}") for q in range(RING2)]
        s_bst = [sem(f"base_stored{q}") for q in range(RING2)]
        s_est = [sem(f"et_stored{q}") for q in range(RING2)]
        s_etl = [sem(f"et_loaded{q}") for q in range(2)]
        s_dslot = sem("dst_slot_ready")
        s_mslot = sem("src_slots_ready")
        s_gath = [sem(f"h_gathered{q}") for q in range(2)]
        s_rep = sem("edge_replicated")
        s_prod = sem("products_ready")
        s_vsum = sem("vector_products_added")
        s_contr = sem("products_contracted")
        s_oper_v = [sem(f"vector_operand_replicated{q}") for q in range(2)]
        s_oper_s = [sem(f"scalar_operands_replicated{q}") for q in range(2)]
        s_aux = sem("aux_in_psum")
        s_auxc = sem("aux_copied")
        s_tp = sem("tensor_product_copied")
        s_md = sem("messages_in_psum")
        s_mdc = sem("messages_copied")
        s_shift = sem("vector_row_shift")
        s_same = sem("same_source_ready")
        s_rows = sem("row_numbers_ready")
        s_scat = sem("scattered")

        def by_partition(ap):
            return ap.rearrange("(p t) c -> p (t c)", t=T)

        def full_columns(ap, width):
            return bass.AP(tensor=ap.tensor, offset=0, ap=[[T * width, P], [1, TAIL * width]])

        def pair(view, width, j):
            return view[:, bass.ds(j * (2 * G * width), 2 * G * width)]

        def slots(buf, q):
            return buf[:, 2 * q:2 * q + 2].rearrange("p a g c -> p (a g c)")

        n_wload = [0]

        def ld(engine, dst_ap, src_ap):
            engine.dma_start(dst_ap, src_ap).then_inc(s_wload, 16)
            n_wload[0] += 16

        def rows_in_order(dst_a, dst_b, mat):
            vec = mat[S0:D, :].rearrange("(c i) n -> c i n", i=3)
            return ((dst_a[0:S0, :], mat[0:S0, :]), (dst_a[S0:S0 + V0, :], vec[:, 0, :]),
                    (dst_a[S0 + V0:P, :], vec[:, 1, :]), (dst_b[0:V0, :], vec[:, 2, :]))

        block = ctx.enter_context(nc.Block())

        @block.sync
        def _(sp):
            inputs = ((x_s, x, D, s_x), (e_s, e, DE, s_e))

            def load(j, q, full, turn=0):
                if after(turn, 1):
                    sp.wait_ge(s_bst[q], turn * 16)
                for buf, ap, width, s in inputs:
                    if full:
                        sp.dma_start(slots(buf, q), pair(full_columns(ap, width), width, j)).then_inc(s[q], 16)
                        sp.sem_inc(s[q], 16)
                    else:
                        head = by_partition(ap[0:(P - 1) * T, :])
                        for p0, p1 in ((0, SPLIT), (SPLIT, P - 1)):
                            sp.dma_start(slots(buf, q)[p0:p1], pair(head[p0:p1], width, j)).then_inc(s[q], 16)

            def store(j, q):
                sp.wait_ge(s_h, j * 2 + 2)
                sp.dma_start(pair(by_partition(h_dram), D, j), slots(h_s, q)).then_inc(s_hst[q], 16)
                sp.wait_ge(s_et, j * 2 + 2)
                sp.dma_start(et_dram.rearrange("(b k) w -> k b w", k=KE)[:, bass.ds(j * 2, 2), :],
                             et_w[:, 2 * q:2 * q + 2, :]).then_inc(s_est[q], 16)
                sp.wait_ge(s_base, j * 2 + 2)
                sp.dma_start(pair(by_partition(out), D, j), slots(x_s, q)).then_inc(s_bst[q], 16)

            def load_product_weights():
                for r in range(4):
                    rows_r = slice(V0 * r, V0 * (r + 1))
                    for j in range(2):
                        ld(sp, w1c[rows_r, j, :, :], w1[:, 4 * j + r, :].rearrange("(h a) c -> a h c", h=2))
                    ld(sp, w2c[rows_r, :, :], w2.rearrange("a (j r) c -> r a j c", r=4)[r])
                    ld(sp, w4c[rows_r, :, :], w4.rearrange("a (j r) c -> r a j c", r=4)[r])

            def load_message_weights():
                ld(sp, w3c[0:S0, :, :], w3.rearrange("a (j b) c -> a j (b c)", j=2))
                for to, rows in rows_in_order(wma, wmb, wm):
                    ld(sp, to, rows)
                ld(sp, wmb[V0:V0 + 1, :], bm.rearrange("(o n) -> o n", o=1))
                ld(sp, wmb[S0:P, :], wm[0:S0, :])
                ld(sp, wub[:, 0, :], wu[D:D + P, :])
                ld(sp, wub[0:D - P, 1, :], wu[D + P:2 * D, :])

            AHEAD = 4

            load(0, 0, True)
            for table, flat in ((src_i, src), (dst_i, dst)):
                if table is src_i:
                    sp.wait_ge(s_pad, 1)
                v = table[:, :, :].rearrange("p b g -> p (b g)")
                head = flat[0:(P - 1) * T].rearrange("(p t) -> p t", t=T)
                sp.dma_start(v[0:SPLIT, :], head[0:SPLIT, :]).then_inc(s_iload, 16)
                sp.dma_start(v[SPLIT:P - 1, :], head[SPLIT:P - 1, :]).then_inc(s_iload, 16)
                sp.dma_start(v[P - 1:P, 0:TAIL], flat[(P - 1) * T:N].rearrange("(p t) -> p t", p=1)).then_inc(s_iload, 16)
            for j in range(1, AHEAD):
                load(j, j, True)
            for j in range(RING2):
                load(j + AHEAD, (j + AHEAD) % RING2, True, (j + AHEAD) // RING2)
                store(j, j)
                if j == 1:
                    load_product_weights()
                if j == 4:
                    sp.wait_ge(s_zero, 2)
                    load_message_weights()
            with sp.Fori(1, 3) as i:
                for q in range(RING2):
                    load(i * RING2 + (q + AHEAD), (q + AHEAD) % RING2, True, i + (q + AHEAD) // RING2)
                    store(i * RING2 + q, q)
            for j in range(3 * RING2, 4 * RING2):
                load(j + AHEAD, (j + AHEAD) % RING2, j + AHEAD < FULL2, (j + AHEAD) // RING2)
                store(j, j % RING2)
            with sp.Fori(4, 6) as i:
                for q in range(RING2):
                    load(i * RING2 + (q + AHEAD), (q + AHEAD) % RING2, False, i + (q + AHEAD) // RING2)
                    store(i * RING2 + q, q)
            for j in range(6 * RING2, NB2):
                if j + AHEAD < NB2:
                    load(j + AHEAD, (j + AHEAD) % RING2, False, (j + AHEAD) // RING2)
                store(j, j % RING2)

            for q in range(RING2):
                sp.wait_ge(s_est[q], 16 * (NB // RING))

            def load_et(k, q):
                sp.dma_start(et[:, q, :], et_dram[bass.ds(k * KE, KE), :]).then_inc(s_etl[q], 16)

            def replicate_operands(k, q):
                sp.wait_ge(s_auxc, k * AUX + 1)
                for s, moves in ((s_oper_v, V_BY_DMA), (s_oper_s, S_BY_DMA)):
                    for slot, row in moves:
                        for r in range(4):
                            sp.dma_start(operand[V0 * r:V0 * (r + 1), q, slot, :],
                                         ht_raw[row:row + V0, :]).then_inc(s[q], 16)

            load_et(0, 0)
            load_et(1, 1)
            replicate_operands(0, 0)
            replicate_operands(1, 1)
            with sp.Fori(1, NB // 2) as i:
                for q in range(2):
                    k = i * 2 + q
                    sp.wait_ge(s_rep, (k - 2) * STEPS + STEPS)
                    load_et(k, q)
                    replicate_operands(k, q)

        @block.gpsimd
        def _(pool):
            pool.memset(ident[:, :], 0.0).then_inc(s_const, 1)
            pool.memset(ident_b[:, :], 0.0).then_inc(s_const, 1)
            pool.memset(pick[:, :], 0.0).then_inc(s_const, 1)
            pool.memset(sum_b[:, :], 0.0).then_inc(s_const, 1)
            pool.memset(upto[:, :], 1.0).then_inc(s_const, 1)
            pool.iota(dump_row[:, :], [[0, 1]], base=DUMP, channel_multiplier=1,
                      allow_small_or_imprecise_dtypes=True).then_inc(s_const, 1)
            pool.wait_ge(s_const, 6)
            for m in (ident, ident_b):
                pool.affine_select(out=m[:, :], in_=m[:, :], compare_op=ALU.not_equal, fill=1.0, base=0,
                                   pattern=[[-1, P]], channel_multiplier=1).then_inc(s_const, 1)
            pool.affine_select(out=upto[:, :], in_=upto[:, :], compare_op=ALU.is_ge, fill=0.0, base=0,
                               pattern=[[-1, P]], channel_multiplier=1).then_inc(s_const, 1)
            for n in range(3):
                pool.affine_select(out=pick[:, :], in_=pick[:, :], compare_op=ALU.not_equal, fill=1.0, base=-DE * n,
                                   pattern=[[-1, DE]], channel_multiplier=1).then_inc(s_const, 1)
                pool.wait_ge(s_const, 10 + n)
            for n in range(4):
                pool.affine_select(out=sum_b[:, :], in_=sum_b[:, :], compare_op=ALU.not_equal, fill=1.0, base=-V0 * n,
                                   pattern=[[-1, V0]], channel_multiplier=1).then_inc(s_const, 1)
                pool.wait_ge(s_const, 13 + n)

            def wait(s, value):
                pool.wait_ge(s, value)
                pool.sem_inc(s_passed, 1)

            def split(b):
                def link(ins, n):
                    ins.then_inc(s_split, 1)
                    wait(s_split, b.g * 4 + n)
                wait(s_e[b.slot2], (b.turn + 1) * 32)
                if after(b.g, 2):
                    wait(s_et_ps, b.g - 1)
                part = ep_s[:, b.par, :, 0:3 * DE].rearrange("p g (n d) -> p g n d", n=3)
                rest, e_in = er_s[:, b.par], e_s[:, b.slot]
                pool.tensor_copy(ep_s[:, b.par, :, SRC_ROW:SRC_ROW + 2],
                                 src_b[:, bass.ds(b.g, 1)].rearrange("p b n g -> p (b g) n"))
                link(pool.tensor_copy(part[:, :, 0, :], e_in), 1)
                link(pool.tensor_tensor(rest, e_in, part[:, :, 0, :], ALU.subtract), 2)
                link(pool.tensor_copy(part[:, :, 1, :], rest), 3)
                link(pool.tensor_tensor(rest, rest, part[:, :, 1, :], ALU.subtract), 4)
                pool.tensor_copy(part[:, :, 2, :], rest).then_inc(s_ep, 1)

            pool.wait_ge(s_tables, 1)
            pass_over_nodes(pool, (split, 0))

            def gather(k, q, t):
                pool.indirect_dma_start(
                    out=hg[:, q, t, :], out_offset=None, in_=h_dram,
                    in_offset=bass.IndirectOffsetOnAxis(ap=dst_slot[:, q, t:t + 1], axis=0),
                ).then_inc(s_gath[q], 16)

            def scatter(k, q, t):
                if t in (0, 2):
                    wait(s_mdc, k * 4 + 3 + t // 2)
                if after(k, 1) or t > 0:
                    wait(s_scat, k * (G * 16) + t * 16)
                pool.indirect_dma_start(
                    out=out, out_offset=bass.IndirectOffsetOnAxis(ap=row_slot[:, q, t:t + 1], axis=0),
                    in_=dd_s[:, q, t, :], in_offset=None, compute_op=ALU.add,
                ).then_inc(s_scat, 16)

            def add_products(k, q, i3, h):
                wait(s_prod, k * STEPS + EV[i3] + 1)
                if i3 == 2:
                    wait(s_vsum, k * ADDS_PER_BLOCK + h + 1)
                to = prod[:, q, FIRST[EV0] + h, :]
                pool.tensor_tensor(to, to, prod[:, q, FIRST[EV[i3]] + h, :], ALU.add).then_inc(s_vsum, 1)

            for q in range(RING2):
                pool.wait_ge(s_hst[q], 16 * (NB // RING))
            for k in range(2):
                wait(s_dslot, k + 1)
                for t in range(G):
                    gather(k, k, t)
            for q in range(RING2):
                pool.wait_ge(s_bst[q], 16 * (NB // RING))

            def edge_block(k, q, with_gather=True, with_products=True):
                if with_gather:
                    wait(s_aux, (k + 1) * AUX)
                    wait(s_dslot, k + 3)
                if after(k, 2):
                    wait(s_rows, k - 1)
                for t in range(G + 1):
                    if with_gather and t < G:
                        gather(k + 2, q, t)
                    if with_products and t in ADDS:
                        for i3, h in ADDS[t]:
                            add_products(k, q, i3, h)
                    if after(k, 2) and t < G:
                        scatter(k - 2, q, t)

            for k in range(4):
                edge_block(k, k % 2)
            with pool.Fori(2, NB // 2 - 1) as i:
                for q in range(2):
                    edge_block(i * 2 + q, q)
            for k in range(NB - 2, NB + 2):
                edge_block(k, k % 2, with_gather=False, with_products=k < NB)
            pool.wait_ge(s_scat, NB * G * 16)

        @block.scalar
        def _(act):
            act.wait_ge(s_zero, 1)
            for to, rows in rows_in_order(wta, wtb, wu[0:D, :]):
                act.dma_start(to, rows).then_inc(s_wuload, 16)
            act.dma_start(wtb[V0:V0 + 1, :], bu.rearrange("(o n) -> o n", o=1)).then_inc(s_wuload, 16)

            def deviation(b):
                act.wait_ge(s_var, b.g + 1)
                if after(b.g, 2):
                    act.wait_ge(s_rstd, b.g - 1)
                nc.scalar.activation(std[:, b.par, :], mv[:, b.par, :, 1], ACT.Sqrt, bias=eps[:, 0:1],
                                     scale=1.0).then_inc(s_std, 1)

            def relu(b):
                act.wait_ge(s_z, b.g + 1)
                if after(b.g, RING):
                    act.wait_ge(s_hst[b.slot2], b.turn * 16)
                nc.scalar.activation(h_s[:, b.slot, :, 0:S0], z_s[:, b.par, :, 0:S0], ACT.Relu)
                nc.scalar.activation(h_s[:, b.slot, :, S0:D].rearrange("p g (i c) -> p g i c", i=3),
                                     z_s[:, b.par, :, S0:D].rearrange("p g (c i) -> p g i c", i=3),
                                     ACT.Relu).then_inc(s_h, 1)

            def copy_transposed(b):
                act.wait_ge(s_ht_ps, b.g + 1)
                if after(b.g, 2):
                    act.wait_ge(s_base_ps, b.g - 1)
                nc.scalar.activation(hta[:, b.par, :], ps[:, b.par, :], ACT.Copy)
                nc.scalar.activation(htb[0:V0, b.par, :], ps[0:V0, 2, :], ACT.Copy).then_inc(s_ht, 1)
                act.wait_ge(s_et_ps, b.g + 1)
                if after(b.g, RING):
                    act.wait_ge(s_est[b.slot2], b.turn * 16)
                nc.scalar.activation(et_w[:, b.slot, :], n_et, ACT.Copy).then_inc(s_et, 1)

            pass_over_nodes(act, (deviation, 0), (copy_transposed, 2), (relu, 1))

            act.wait_ge(s_wt_ps, 1)
            nc.scalar.activation(wmta[:, :, :], ps[:, 0, 0:2 * P].rearrange("p (a b) -> p a b", a=2), ACT.Copy)
            nc.scalar.activation(wmtb[0:V0, :, :], ps[0:V0, 1, 0:2 * P].rearrange("p (a b) -> p a b", a=2),
                                 ACT.Copy).then_inc(s_wt_sb, 1)
            act.wait_ge(s_wt_ps, 2)
            nc.scalar.activation(wfa[:, :], ps[:, 2, 0:D], ACT.Copy)
            nc.scalar.activation(wfb[:, :], ps[:, 3, 0:D], ACT.Copy).then_inc(s_wt_sb, 1)

            act.wait_ge(s_tables, 1)
            act.wait_ge(s_iload, 96)

            def slot_dst(k, q):
                nc.scalar.activation(dst_slot[:, q, :], dst_i[:, bass.ds(k, 1), :].rearrange("p b g -> p (b g)"),
                                     ACT.Copy).then_inc(s_dslot, 1)

            def slot_src(k, q):
                nc.scalar.activation(srcf_slot[:, q].rearrange("p a g -> p (a g)"),
                                     src_f[:, bass.ds(k, 1)].rearrange("p b a g -> p (b a g)"),
                                     ACT.Copy).then_inc(s_mslot, 1)

            def copy_aux(k, q, n, turn):
                act.wait_ge(s_aux, k * AUX + n + 1)
                if n == 0:
                    if after(k, 1):
                        act.wait_ge(s_oper_v[1 - q], (turn + 1) * (4 * len(V_BY_DMA) * 16))
                        act.wait_ge(s_oper_s[1 - q], (turn + 1) * (4 * len(S_BY_DMA) * 16))
                    if after(k, 2):
                        act.wait_ge(s_prod, (k - 1) * STEPS)
                    nc.scalar.activation(ht_raw[:, :], ps[:, 6, :], ACT.Copy).then_inc(s_auxc, 1)
                elif n == 3:
                    for r in range(4):
                        last = nc.scalar.activation(operand[V0 * r:V0 * (r + 1), q, XV + 2, :], ps[0:V0, 6, :], ACT.Copy)
                    last.then_inc(s_auxc, 1)
                else:
                    nc.scalar.activation(operand[:, q, Y3 + n - 1, :], ps[:, 6, :], ACT.Copy).then_inc(s_auxc, 1)

            def copy_v1(k, q):
                act.wait_ge(s_auxc, k * AUX + 1)
                for r in range(4):
                    nc.scalar.activation(operand[V0 * r:V0 * (r + 1), q, XV + 1, :], ht_raw[S0 + V0:P, :], ACT.Copy)

            def copy_md(k, q, n):
                act.wait_ge(s_md, k * 4 + n + 1)
                if n == 2 and after(k, 2):
                    act.wait_ge(s_scat, (k - 1) * (G * 16))
                j = n % 2
                dest = m_s[:, 2 * j:2 * j + 2, :] if n < 2 else dd_s[:, q, 2 * j:2 * j + 2, :]
                nc.scalar.activation(dest, ps[:, 7, 0:2 * D].rearrange("p (a b) -> p a b", a=2), ACT.Copy).then_inc(s_mdc, 1)

            def copy_tp(k):
                act.wait_ge(s_contr, k + 1)
                if after(k, 1):
                    act.wait_ge(s_md, (k - 1) * 4 + 2)
                for h in range(2):
                    cols = slice(h * (W // 2), (h + 1) * (W // 2))
                    nc.scalar.activation(tp[:, :, cols], ps[:, 4:6, cols], ACT.Copy).then_inc(s_tp, 1)

            def edge_block(k, q, c, nxt=True, nxt3=True):
                o = 1 - q
                prev = after(k, 1)
                if prev:
                    copy_tp(k - 1)
                if nxt:
                    if prev:
                        act.wait_ge(s_same, k)
                    slot_src(k + 1, o)
                for u in range(STEPS):
                    if u in MD_STEP:
                        ago, n = MD_STEP[u]
                        if after(k, ago):
                            copy_md(k - ago, o if ago == 1 else q, n)
                    if nxt and u in AUX_STEP:
                        copy_aux(k + 1, o, AUX_STEP[u], c)
                    if nxt and u == 2:
                        copy_v1(k + 1, o)
                if nxt3:
                    act.wait_ge(s_aux, (k + 2) * AUX)
                    slot_dst(k + 3, o)

            slot_dst(0, 0)
            slot_dst(1, 1)
            slot_src(0, 0)
            copy_aux(0, 0, 0, None)
            copy_v1(0, 0)
            for n in range(1, AUX):
                copy_aux(0, 0, n, None)
            slot_dst(2, 0)
            edge_block(0, 0, 0)
            edge_block(1, 1, 0)
            with act.Fori(1, NB // 2 - 2) as i:
                for q in range(2):
                    edge_block(i * 2 + q, q, i)
            for k in range(NB - 4, NB):
                edge_block(k, k % 2, k // 2, nxt=(k + 1 < NB), nxt3=(k + 3 < NB))
            copy_tp(NB - 1)
            copy_md(NB - 2, 0, 3)
            for n in range(4):
                copy_md(NB - 1, 1, n)

        @block.vector
        def _(dve):
            v = nc.vector
            v.memset(wtb[:, :], 0.0).then_inc(s_zero, 1)
            for m in (w3c[:, :, :], wmb[:, :], wub[:, :, :], wmtb[:, :, :]):
                last = v.memset(m, 0.0)
            last.then_inc(s_zero, 1)
            for m, value in ((htb[:, :, :], 0.0), (perm_a[:, :], 0.0), (perm_b[:, :], 0.0),
                             (eps[:, :], EPS), (dst_i[:, :, :], 0), (ep_s[:, :, :, :], 0.0),
                             (rep[:, 8, :], 0.0)):
                last = v.memset(m, value)
            last.then_inc(s_prep, 1)
            dve.wait_ge(s_const, 6)
            v.tensor_scalar(src_i[:, :, :].rearrange("p b g -> p (b g)"),
                            dump_row[:, 0:1].to_broadcast([P, T]), 0.0, None, ALU.add).then_inc(s_pad, 1)
            dve.wait_ge(s_prep, 1)
            v.memset(htb[V0:V0 + 1, :, :], 1.0)
            dve.wait_ge(s_const, 9)
            v.tensor_copy(perm_a[0:S0, 0:S0], ident[0:S0, 0:S0])
            for m, r0, i3 in ((perm_a, S0, 0), (perm_a, S0 + V0, 1), (perm_b, 0, 2)):
                last = v.tensor_copy(m[r0:r0 + V0, S0:D].rearrange("r (c i) -> r i c", i=3)[:, i3, :],
                                     ident[r0:r0 + V0, r0:r0 + V0])
            last.then_inc(s_prep, 1)
            dve.wait_ge(s_prep, 2)
            dve.wait_ge(s_iload, 96)
            v.tensor_copy(src_f[:, :, 0, :], src_i[:, :, :])
            v.tensor_scalar(part_i[:, 0], src_i[:, :, :], 8, 8, ALU.logical_shift_right, ALU.logical_shift_left)
            v.tensor_scalar(part_i[:, 1], src_i[:, :, :], 255, None, ALU.bitwise_and).then_inc(s_prep, 1)
            dve.wait_ge(s_prep, 3)
            v.tensor_scalar(src_f[:, :, 1, :], src_f[:, :, 0, :], -1.0, dump_row[:, 0:1], ALU.mult, ALU.add)
            v.tensor_copy(src_b[:, :, 0, :], part_i[:, 0])
            v.tensor_copy(src_b[:, :, 1, :], part_i[:, 1]).then_inc(s_tables, 1)
            dve.wait_ge(s_wuload, 80)
            v.tensor_tensor(wta[:, :], wta[:, :], perm_a[:, :], ALU.add)
            v.tensor_tensor(wtb[0:V0, :], wtb[0:V0, :], perm_b[:, :], ALU.add).then_inc(s_wt, 1)
            dve.wait_ge(s_const, 12)
            for r in range(8):
                if r < 2:
                    cols = pick[:, 4 * r:4 * r + 4]
                else:
                    i3, j = (r - 2) // 2, (r - 2) % 2
                    cols = pick[:, EB:DE].rearrange("k (b i) -> k i b", i=3)[:, i3, 4 * j:4 * j + 4]
                v.tensor_copy(rep[:, r, :].rearrange("k (b a) -> k b a", a=V0),
                              cols[:, :, None].to_broadcast([KE, 4, V0]))
            v.memset(rep[SRC_ROW:SRC_ROW + 2, 8, :], 1.0)

            def statistics(b):
                dve.wait_ge(s_x[b.slot2], (b.turn + 1) * 32)
                for t in range(G):
                    last = v.bn_stats(out=stats[:, b.par, t, :], in_=x_s[:, b.slot, t, :])
                last.then_inc(s_stat, 1)

            def aggregate(b):
                dve.wait_ge(s_stat, b.g + 1)
                dve.sem_inc(s_passed_v, 1)
                for t in range(G):
                    last = v.bn_aggr(out=mv[:, b.par, t, :], in_=stats[:, b.par, t, :])
                last.then_inc(s_var, 1)

            def invert(b):
                dve.wait_ge(s_std, b.g + 1)
                v.reciprocal(rstd[:, b.par, :], std[:, b.par, :]).then_inc(s_rstd, 1)

            def normalise(b):
                dve.wait_ge(s_rstd, b.g + 1)
                if after(b.g, 2):
                    dve.wait_ge(s_h, b.g - 1)
                for t in range(G):
                    last = v.tensor_scalar(z_s[:, b.par, t, :], x_s[:, b.slot, t, :], mv[:, b.par, t, 0:1],
                                           rstd[:, b.par, t:t + 1], ALU.subtract, ALU.mult)
                last.then_inc(s_z, 1)

            def add_base(b):
                dve.wait_ge(s_base_ps, b.g + 1)
                for j in range(2):
                    last = v.tensor_tensor(x_s[:, b.slot, 2 * j:2 * j + 2, :],
                                           ps[:, 3 + 2 * b.par + j, 0:2 * D].rearrange("p (a b) -> p a b", a=2),
                                           x_s[:, b.slot, 2 * j:2 * j + 2, :], ALU.add)
                last.then_inc(s_base, 1)

            pass_over_nodes(dve, (statistics, 0), (invert, 1), (aggregate, 0), (normalise, 1), (add_base, 4))

            dve.wait_ge(s_base, NB)
            v.memset(ps[V0:S0, 5, :], 0.0).then_inc(s_prep, 1)
            dve.wait_ge(s_prep, 4)
            v.memset(ps[V0:V0 + 1, 5, :], 1.0)
            dve.wait_ge(s_wload, n_wload[0])
            half = 0.5 ** 0.5
            for m, scale in ((w1c[:, :, :, :], (S0 * EB) ** -0.5 * half), (w2c[:, :, :], (3.0 * V0 * EB) ** -0.5 * half),
                             (w4c[:, :, :], (V0 * EB) ** -0.5 * half), (w3c[:, :, :], (S0 * EB) ** -0.5 * half)):
                last = v.tensor_scalar(m, m, scale, None, ALU.mult)
            last.then_inc(s_scaled, 1)

            def products(k, q, c, u):
                dve.wait_ge(s_rep, k * STEPS + u + 1)
                if u == EV0:
                    dve.wait_ge(s_oper_v[q], (c + 1) * (4 * len(V_BY_DMA) * 16))
                    if after(k, 2):
                        dve.wait_ge(s_contr, k - 1)
                if u == OWNERS + 1:
                    dve.wait_ge(s_auxc, (k + 1) * AUX)
                if u == ES0:
                    dve.wait_ge(s_oper_s[q], (c + 1) * (4 * len(S_BY_DMA) * 16))
                banks = pair_of(u)
                op = operand[:, q]
                f = FIRST[u]
                if u in (ES0, ES1):
                    last = v.tensor_tensor(prod[:, q, f:f + 5, :], op[:, XS:XS + 5, :],
                                           banks[:, 0:1, :].to_broadcast([P, 5, W]), ALU.mult)
                else:
                    i3 = EV.index(u)
                    v.tensor_tensor(prod[:, q, f:f + 2, :], op[:, XV + i3:XV + i3 + 1, :].to_broadcast([P, 2, W]),
                                    banks, ALU.mult)
                    if u == EV0:
                        dve.wait_ge(s_auxc, k * AUX + 3)
                    last = v.tensor_tensor(prod[:, q, f + 2:f + 4, :], op[:, Y3:Y3 + 2, :], banks, ALU.mult)
                last.then_inc(s_prod, 1)

            def owners(k, q):
                dve.wait_ge(s_rep, k * STEPS + OWNERS + 1)
                dve.wait_ge(s_mslot, k + 1)
                if after(k, 2):
                    dve.wait_ge(s_md, (k - 2) * 4 + 4)
                for t in range(G):
                    last = v.scalar_tensor_tensor(out=same[:, q, t, :], in0=pair_of(OWNERS)[:, 0, P * t:P * (t + 1)],
                                                  scalar=srcf_slot[:, q, 0, t:t + 1], in1=upto[:, :],
                                                  op0=ALU.is_equal, op1=ALU.mult, accum_out=count[:, t:t + 1])
                last.then_inc(s_prod, 1)
                dve.wait_ge(s_prod, k * STEPS + OWNERS + 1)
                v.scalar_tensor_tensor(out=shift[:, :], in0=count[:, :], scalar=1.5, in1=srcf_slot[:, q, 1, :],
                                       op0=ALU.is_gt, op1=ALU.mult).then_inc(s_shift, 1)
                dve.wait_ge(s_shift, k + 1)
                v.tensor_tensor(row_f[:, q, :], shift[:, :], srcf_slot[:, q, 0, :], ALU.add).then_inc(s_same, 1)

            def row_numbers(k, q):
                dve.wait_ge(s_same, k + 1)
                if after(k, 2):
                    dve.wait_ge(s_scat, (k - 1) * (G * 16))
                v.tensor_copy(row_slot[:, q, :], row_f[:, q, :]).then_inc(s_rows, 1)

            def edge_block(k, q, c):
                for u in range(STEPS):
                    if u == OWNERS:
                        owners(k, q)
                    else:
                        products(k, q, c, u)
                    if u == OWNERS + 1 and after(k, 1):
                        row_numbers(k - 1, 1 - q)

            for k in range(2):
                edge_block(k, k, 0)
            with dve.Fori(1, NB // 2) as i:
                for q in range(2):
                    edge_block(i * 2 + q, q, i)
            row_numbers(NB - 1, 1)

        @block.tensor
        def _(pe):
            mm = nc.tensor.matmul
            pe.wait_ge(s_const, 16)
            pe.wait_ge(s_wt, 1)

            def transposes(b):
                pe.wait_ge(s_h, b.g + 1)
                if after(b.g, 1):
                    pe.wait_ge(s_ht, b.g)
                for t in range(G):
                    nc.tensor.transpose(ps[:, b.par, P * t:P * (t + 1)], h_s[:, b.slot, t, 0:P], ident[:, :])
                for t in range(G):
                    last = nc.tensor.transpose(ps[0:V0, 2, P * t:P * (t + 1)], h_s[:, b.slot, t, P:D], ident[:, :])
                last.then_inc(s_ht_ps, 1)
                pe.wait_ge(s_ep, b.g + 1)
                if after(b.g, 1):
                    pe.wait_ge(s_et, b.g)
                for t in range(G):
                    last = nc.tensor.transpose(n_et[:, P * t:P * (t + 1)],
                                               ep_s[:, b.par, t, :], ident_b[:, :])
                last.then_inc(s_et_ps, 1)

            def product(b):
                pe.wait_ge(s_ht, b.g + 1)
                if after(b.g, 2):
                    pe.wait_ge(s_base, b.g - 1)
                for t in range(G):
                    o = ps[:, 3 + 2 * b.par + t // 2, D * (t % 2):D * (t % 2 + 1)]
                    mm(o, hta[:, b.par, P * t:P * (t + 1)], wta[:, :], start=True, stop=False)
                    last = mm(o, htb[:, b.par, P * t:P * (t + 1)], wtb[:, :], start=False, stop=True)
                last.then_inc(s_base_ps, 1)

            pass_over_nodes(pe, (product, 2), (transposes, 0))

            pe.wait_ge(s_base, NB)
            pe.wait_ge(s_et, NB)
            pe.wait_ge(s_wload, n_wload[0])
            for n, m in enumerate((wma, wmb)):
                nc.tensor.transpose(ps[:, 0, P * n:P * (n + 1)], m[:, 0:P], ident[:, :])
                last = nc.tensor.transpose(ps[0:D - P, 1, P * n:P * (n + 1)], m[:, P:D], ident[:, :])
            last.then_inc(s_wt_ps, 1)
            pe.wait_ge(s_wt_sb, 1)
            for n in range(2):
                mm(ps[:, 2 + n, 0:D], wmta[:, n, :], wub[:, 0, :], start=True, stop=False)
                last = mm(ps[:, 2 + n, 0:D], wmtb[:, n, :], wub[:, 1, :], start=False, stop=True)
            last.then_inc(s_wt_ps, 1)
            pe.wait_ge(s_wt_sb, 2)
            pe.wait_ge(s_scaled, 1)


            def aux(k, q, c, n):
                if after(k, 1) or n > 0:
                    pe.wait_ge(s_auxc, k * AUX + n)
                if n == 0:
                    pe.wait_ge(s_gath[q], (c + 1) * (G * 16))
                    for t in range(G):
                        r = nc.tensor.transpose(ps[:, 6, P * t:P * (t + 1)], hg[:, q, t, 0:P], ident[:, :])
                elif n == 3:
                    for t in range(G):
                        r = nc.tensor.transpose(ps[0:V0, 6, P * t:P * (t + 1)], hg[:, q, t, P:D], ident[:, :])
                else:
                    r = mm(ps[:, 6, :], w3c[:, n - 1, :], ht_raw[:, :], start=True, stop=True)
                r.then_inc(s_aux, 1)

            def replicate(k, q, c, u):
                if u == 0:
                    pe.wait_ge(s_etl[q], (c + 1) * 16)
                if after(k, 1) or u >= 2:
                    pe.wait_ge(s_prod, k * STEPS + u - 1)
                banks = pair_of(u)
                for j, r in enumerate(REPS[u]):
                    last = mm(banks[:, j, :], rep[:, r, :], et[:, q, :], start=True, stop=True)
                last.then_inc(s_rep, 1)

            tp_s = [ps[0:S0, 4, :], ps[S0:P, 5, :]]
            tp_v = [ps[S0:S0 + V0, 4, :], ps[S0 + V0:P, 4, :], ps[0:V0, 5, :]]

            def contract(k, q, u):
                pe.wait_ge(s_prod, k * STEPS + u + 1)
                pr = prod[:, q]
                if u == EV2:
                    for h in range(2):
                        for i3 in range(3):
                            mm(tp_v[i3], sum_b[:, :], pr[:, FIRST[EV[i3]] + 2 + h, :], start=False, stop=False)
                else:
                    if u == ES0 and after(k, 1):
                        pe.wait_ge(s_tp, k * 2)
                    n = (ES0, ES1).index(u)
                    for h in range(2):
                        mm(tp_s[h], w1c[:, n, h, :], pr[:, FIRST[u] + h, :], start=(u == ES0), stop=(u == ES1))
                    for i3 in range(3):
                        last = mm(tp_v[i3], w4c[:, n, :], pr[:, FIRST[u] + 2 + i3, :], start=(u == ES0), stop=(u == ES1))
                    if u == ES1:
                        last.then_inc(s_contr, 1)

            def contract_added(k, q):
                pe.wait_ge(s_vsum, (k + 1) * ADDS_PER_BLOCK)
                for h in range(2):
                    mm(tp_s[h], w2c[:, h, :], prod[:, q, FIRST[EV0] + h, :], start=False, stop=False)

            def messages(k, q, n):
                if n < 2:
                    pe.wait_ge(s_tp, k * 2 + n + 1)
                if n > 0 or after(k, 1):
                    pe.wait_ge(s_mdc, k * 4 + n)
                for t in (2 * (n % 2), 2 * (n % 2) + 1):
                    o = ps[:, 7, D * (t % 2):D * (t % 2 + 1)]
                    if n < 2:
                        mm(o, tp[:, 0, P * t:P * (t + 1)], wfa[:, :], start=True, stop=False)
                        last = mm(o, tp[:, 1, P * t:P * (t + 1)], wfb[:, :], start=False, stop=True)
                    else:
                        last = mm(o, same[:, q, t, :], m_s[:, t, :], start=True, stop=True)
                last.then_inc(s_md, 1)

            def edge_block(k, q, c, nxt=True):
                o = 1 - q
                for u in range(STEPS):
                    if u + 1 < STEPS:
                        replicate(k, q, c, u + 1)
                    elif nxt:
                        replicate(k + 1, o, c + q, 0)
                    if u == 0 and after(k, 1):
                        contract_added(k - 1, o)
                        contract(k - 1, o, ES1)
                    if u in CONTRACT:
                        contract(k, q, CONTRACT[u])
                    if u in MD_STEP:
                        ago, n = MD_STEP[u]
                        if after(k, ago):
                            messages(k - ago, o if ago == 1 else q, n)
                    if nxt and u in AUX_STEP:
                        aux(k + 1, o, c + q, AUX_STEP[u])

            for n in range(AUX):
                aux(0, 0, 0, n)
            replicate(0, 0, 0, 0)
            edge_block(0, 0, 0)
            edge_block(1, 1, 0)
            with pe.Fori(1, NB // 2 - 1) as i:
                for q in range(2):
                    edge_block(i * 2 + q, q, i)
            edge_block(NB - 2, 0, NB // 2 - 1)
            edge_block(NB - 1, 1, NB // 2 - 1, nxt=False)
            contract_added(NB - 1, 1)
            contract(NB - 1, 1, ES1)
            messages(NB - 2, 0, 3)
            for n in range(4):
                messages(NB - 1, 1, n)


_INS = ["x", "src", "dst", "edge_attr_32", "L0_gnn_W1", "L0_gnn_W2", "L0_gnn_W3", "L0_gnn_W4", "L0_gnn_Wm",
        "L0_gnn_bm", "L0_gnn_Wu", "L0_gnn_bu"]


def kernel(**inputs):
    import numpy as np
    import concourse.bacc as bacc
    from concourse.bass_utils import run_bass_kernel_spmd

    nc = bacc.Bacc("TRN2", target_bir_lowering=False, num_devices=1)
    arrays, args = {}, []
    for name in _INS:
        a = np.ascontiguousarray(inputs[name])
        arrays[f"in_{name}"] = a
        args.append(nc.dram_tensor(f"in_{name}", a.shape, mybir.dt.from_np(a.dtype), kind="ExternalInput").ap())
    out = nc.dram_tensor("out_rows", (NPAD, D), F32, kind="ExternalOutput").ap()
    tp_message_passing(nc, *args, out)
    r = run_bass_kernel_spmd(nc, [arrays], core_ids=[0])
    return r.results[0]["out_rows"][0:N]
```
